# Optimizing a Trainium2 kernel written in Bass

```python
import numpy as np
import jax
import jax.numpy as jnp

def _softmax(x, axis=-1):
    return jax.nn.softmax(x, axis=axis)

def _gelu(x):
    return jax.nn.gelu(x, approximate=True)

def _silu(x):
    return jax.nn.silu(x)

def _sigmoid(x):
    return jax.nn.sigmoid(x)

def _layernorm(x, axis=-1, eps=1e-05):
    m = jnp.mean(x, axis=axis, keepdims=True)
    v = jnp.var(x, axis=axis, keepdims=True)
    return (x - m) / jnp.sqrt(v + eps)

def _scatter_add(tgt, idx, src, axis=0):
    return tgt.at[idx].add(src)

def _segment_sum(src, seg, n):
    return jax.ops.segment_sum(src, seg, n)
kernel_name = 'mk_adaln_ffn_d1_seqx_r8_b13512'

def setup_inputs(seed: int=0):
    np.random.seed(seed)
    _w = jnp.asarray

    def _rec_inputs():
        import jax
        import jax.numpy as jnp
        _rk = jax.random.key(seed)
        x = 8.748e-05 + 1 * jax.random.normal(jax.random.fold_in(_rk, 1), (32, 32, 256), jnp.float32)
        _lenS = 32 - jax.random.randint(jax.random.fold_in(_rk, 7), (32,), 0, max(1, 32 // 4) + 1, jnp.int32)
        _lenS2 = 32 - jax.random.randint(jax.random.fold_in(_rk, 8), (32,), 0, max(1, 32 // 4) + 1, jnp.int32)
        cond_2048 = -9.80646e-05 + 1.00041 * jax.random.normal(jax.random.fold_in(_rk, 11), (32, 256), jnp.float32)
        return (x, cond_2048)
    x, cond_2048 = _rec_inputs()

    def _L0_cond_setup():
        import jax, jax.numpy as jnp
        import numpy as np
        DT = 0.01
        EPSILON = 0.08
        ALPHA = 0.7
        BETA = 0.8
        CLAMP = 20.0
        B, T, N = (32, 128, 256)

        def _derivative(q, p, drive, coupling, bias):
            i_couple = jnp.tanh(q) @ coupling.T
            dq = q - q ** 3 / 3.0 - p + drive + i_couple + bias
            dp = EPSILON * (q + ALPHA - BETA * p)
            return (dq, dp)

        def _rk4_step(q, p, drive, coupling, bias):
            dq1, dp1 = _derivative(q, p, drive, coupling, bias)
            dq2, dp2 = _derivative(q + 0.5 * DT * dq1, p + 0.5 * DT * dp1, drive, coupling, bias)
            dq3, dp3 = _derivative(q + 0.5 * DT * dq2, p + 0.5 * DT * dp2, drive, coupling, bias)
            dq4, dp4 = _derivative(q + DT * dq3, p + DT * dp3, drive, coupling, bias)
            q_next = q + DT / 6.0 * (dq1 + 2 * dq2 + 2 * dq3 + dq4)
            p_next = p + DT / 6.0 * (dp1 + 2 * dp2 + 2 * dp3 + dp4)
            q_next = jnp.clip(q_next, -CLAMP, CLAMP)
            p_next = jnp.clip(p_next, -CLAMP, CLAMP)
            return (q_next, p_next)
        key = jax.random.key(seed)
        k1, k2, k3, k4 = jax.random.split(key, 4)
        return {'q0': jax.random.normal(k1, (B, N), dtype=jnp.float32), 'p0': jax.random.normal(k2, (B, N), dtype=jnp.float32), 'input_drive_seq': jax.random.normal(k3, (B, T, N), dtype=jnp.float32), 'coupling': jax.random.normal(k4, (N, N), dtype=jnp.float32) * 0.01, 'bias': jnp.zeros((N,), dtype=jnp.float32)}
    _L0_cond_all = _L0_cond_setup()
    _L0_cond_in = {k: v for k, v in _L0_cond_all.items() if k in ('coupling', 'bias')}
    del _L0_cond_all

    def _L0_ffn_setup():
        import jax, jax.numpy as jnp
        import numpy as np
        B, S, H = (1, 128, 256)
        E = 32
        K = 4
        I = 96
        SI = 512
        WSCALE = 0.02
        key = jax.random.key(seed)
        ks = jax.random.split(key, 8)
        inp = {'hidden_states': jax.random.normal(ks[0], (B, S, H), jnp.float32), 'router_w': jax.random.normal(ks[1], (H, E), jnp.float32) * WSCALE, 'w_gate': jax.random.normal(ks[2], (E, H, I), jnp.float32) * WSCALE, 'w_up': jax.random.normal(ks[3], (E, H, I), jnp.float32) * WSCALE, 'w_down': jax.random.normal(ks[4], (E, I, H), jnp.float32) * WSCALE, 'ws_gate': jax.random.normal(ks[5], (H, SI), jnp.float32) * WSCALE, 'ws_up': jax.random.normal(ks[6], (H, SI), jnp.float32) * WSCALE, 'ws_down': jax.random.normal(ks[7], (SI, H), jnp.float32) * WSCALE}
        return inp
    _L0_ffn_all = _L0_ffn_setup()
    _L0_ffn_in = {k: v for k, v in _L0_ffn_all.items() if k in ('router_w', 'w_gate', 'w_up', 'w_down', 'ws_gate', 'ws_up', 'ws_down')}
    del _L0_ffn_all
    return {'x': x, 'cond_2048': cond_2048, 'L0_cond_coupling': _L0_cond_in['coupling'], 'L0_cond_bias': _L0_cond_in['bias'], 'L0_ffn_router_w': _L0_ffn_in['router_w'], 'L0_ffn_w_gate': _L0_ffn_in['w_gate'], 'L0_ffn_w_up': _L0_ffn_in['w_up'], 'L0_ffn_w_down': _L0_ffn_in['w_down'], 'L0_ffn_ws_gate': _L0_ffn_in['ws_gate'], 'L0_ffn_ws_up': _L0_ffn_in['ws_up'], 'L0_ffn_ws_down': _L0_ffn_in['ws_down']}

def reference(x, cond_2048, L0_cond_coupling, L0_cond_bias, L0_ffn_router_w, L0_ffn_w_gate, L0_ffn_w_up, L0_ffn_w_down, L0_ffn_ws_gate, L0_ffn_ws_up, L0_ffn_ws_down):
    import jax
    import jax.numpy as jnp

    def _L0_cond_ref(q0, p0, input_drive_seq, coupling, bias):
        import jax, jax.numpy as jnp
        import numpy as np
        DT = 0.01
        EPSILON = 0.08
        ALPHA = 0.7
        BETA = 0.8
        CLAMP = 20.0
        B, T, N = (32, 128, 256)

        def _derivative(q, p, drive, coupling, bias):
            i_couple = jnp.tanh(q) @ coupling.T
            dq = q - q ** 3 / 3.0 - p + drive + i_couple + bias
            dp = EPSILON * (q + ALPHA - BETA * p)
            return (dq, dp)

        def _rk4_step(q, p, drive, coupling, bias):
            dq1, dp1 = _derivative(q, p, drive, coupling, bias)
            dq2, dp2 = _derivative(q + 0.5 * DT * dq1, p + 0.5 * DT * dp1, drive, coupling, bias)
            dq3, dp3 = _derivative(q + 0.5 * DT * dq2, p + 0.5 * DT * dp2, drive, coupling, bias)
            dq4, dp4 = _derivative(q + DT * dq3, p + DT * dp3, drive, coupling, bias)
            q_next = q + DT / 6.0 * (dq1 + 2 * dq2 + 2 * dq3 + dq4)
            p_next = p + DT / 6.0 * (dp1 + 2 * dp2 + 2 * dp3 + dp4)
            q_next = jnp.clip(q_next, -CLAMP, CLAMP)
            p_next = jnp.clip(p_next, -CLAMP, CLAMP)
            return (q_next, p_next)
        drive_tbn = jnp.swapaxes(input_drive_seq, 0, 1)

        def scan_fn(carry, drive):
            q, p = carry
            q, p = _rk4_step(q, p, drive, coupling, bias)
            return ((q, p), q)
        (_, _), q_trace_tbn = jax.lax.scan(scan_fn, (q0, p0), drive_tbn)
        return jnp.swapaxes(q_trace_tbn, 0, 1)

    def _L0_ffn_ref(hidden_states, router_w, w_gate, w_up, w_down, ws_gate, ws_up, ws_down):
        import jax, jax.numpy as jnp
        import numpy as np
        B, S, H = (1, 128, 256)
        E = 32
        K = 4
        I = 96
        SI = 512
        WSCALE = 0.02
        b, s, h = hidden_states.shape
        x = hidden_states.reshape(-1, h)
        T = x.shape[0]
        shared = jax.nn.silu(x @ ws_gate) * (x @ ws_up) @ ws_down
        logits = x @ router_w
        probs = jax.nn.softmax(logits.astype(jnp.float32), axis=-1)
        topw, topi = jax.lax.top_k(probs, K)
        topw = topw / jnp.sum(topw, axis=-1, keepdims=True)
        topw = topw.astype(hidden_states.dtype)
        combine = jnp.zeros((T, E), hidden_states.dtype).at[jnp.arange(T)[:, None], topi].add(topw)
        g = jnp.einsum('th,ehi->eti', x, w_gate)
        u = jnp.einsum('th,ehi->eti', x, w_up)
        hmid = jax.nn.silu(g) * u
        routed = jnp.einsum('eti,te,eih->th', hmid, combine, w_down)
        return (shared + routed).reshape(b, s, h)
    x = x + _L0_ffn_ref(_L0_cond_ref(cond_2048, cond_2048, x, L0_cond_coupling, L0_cond_bias), L0_ffn_router_w, L0_ffn_w_gate, L0_ffn_w_up, L0_ffn_w_down, L0_ffn_ws_gate, L0_ffn_ws_up, L0_ffn_ws_down)
    return x

_drawn_inputs = setup_inputs


def setup_inputs(seed=0):
    import zlib

    import numpy as np

    out = dict(_drawn_inputs(seed))
    spreads = {'L0_cond_bias': (0.0, 0.8)}
    factors = {'cond_2048': 2.973,
     'L0_cond_coupling': 8.0,
     'L0_ffn_router_w': 8.0,
     'L0_ffn_w_gate': 8.0,
     'L0_ffn_w_up': 8.0,
     'L0_ffn_w_down': 8.0,
     'L0_ffn_ws_gate': 3.049,
     'L0_ffn_ws_up': 2.955,
     'L0_ffn_ws_down': 3.012}
    for name, (base, spread) in spreads.items():
        noise = np.random.default_rng([zlib.crc32(name.encode()), seed]).standard_normal(out[name].shape)
        drawn = base * np.exp(spread * noise) if base else spread * noise
        out[name] = jnp.asarray(drawn.astype(out[name].dtype))
    for name, factor in factors.items():
        out[name] = (out[name] * factor).astype(out[name].dtype)
    return out
```

```python
import concourse.bass as bass
from concourse import mybir
from contextlib import ExitStack

F32 = mybir.dt.float32
F16 = mybir.dt.float16
ALU = mybir.AluOpType
ACT = mybir.ActivationFunctionType

P = 128
B, T, H = 32, 32, 256
E, I, SI, TOPK = 32, 96, 512, 4
NH = H // P
SPC = P // B
NC = T // SPC
SW = NH * B
GT = 4
GC = GT * P
NG = (E * I + SI) // GC
NGR = E * I // GC
UW = 8 * I
NU = E // 8 + 1
NCONV = 3 * NH * NU
HID = NG * GC
STG = 4 * SPC

DT, EPS, ALPHA, BETA, CLAMP = 0.01, 0.08, 0.7, 0.8, 20.0
CQ = [DT / 2, DT / 2, DT, DT / 6]
CP = [v * EPS for v in CQ]
CPSUM = [DT / 6 * EPS * w for w in (1, 2, 2, 1)]
PSHIFT = ALPHA / BETA

WSCALE = 16.0
CSCALE = 1024.0
HSCALE = 1.0 / (WSCALE * CSCALE * 16.0)
LOW = -1.0e30
HIGH = 1.0e30


def build(nc, x, cond, coupling, bias, router_w, w_gate, w_up, w_down, ws_gate, ws_up, ws_down, unit_of, out):
    ctx = ExitStack()
    with ctx:
        def sb(name, shape, dt=F32):
            return ctx.enter_context(nc.sbuf_tensor(name, shape, dt))

        def pb(name, shape, dt=F32):
            return ctx.enter_context(nc.psum_tensor(name, shape, dt))

        def sem(name):
            return ctx.enter_context(nc.semaphore(name))

        x_tok = sb("x_tok", [P, NC, H])
        drive = sb("drive", [P, NC, NH, SPC, B])
        drive_now = sb("drive_now", [P, NH, SPC, B])
        bias_col = sb("bias_col", [P, NH])
        bias_dt = sb("bias_dt", [P, NH])
        cond_row = sb("cond_row", [B, H])
        coup_row = sb("coup_row", [P, NH, H])
        coupT = sb("coupT", [P, NH, H])
        router = sb("router", [P, NH, E])
        identf = sb("identf", [P, P])
        ident16 = sb("ident16", [P, P], F16)
        selector = sb("selector", [P, HID], F16)

        q_new = sb("q_new", [P, NH, SPC, B])
        q_raw = sb("q_raw", [P, NH, B])
        q_hi = sb("q_hi", [P, NH, SPC, B], F16)
        q_lo = sb("q_lo", [P, NH, SPC, B], F16)
        tok_hi = sb("tok_hi", [P, NH, SPC * B], F16)
        tok_lo = sb("tok_lo", [P, NH, SPC * B], F16)
        y = sb("y", [P, 3, NH, B])
        th = sb("th", [P, NH, B])
        sq = sb("sq", [P, NH, B])
        cubic = sb("cubic", [P, NH, B])
        base = sb("base", [P, NH, B])
        base3 = sb("base3", [P, NH, B])
        qdp = sb("qdp", [P, NH, B])
        qd_half = sb("qd_half", [P, NH, B])
        qd_full = sb("qd_full", [P, NH, B])
        dq = sb("dq", [P, 3, NH, B])
        dsum = sb("dsum", [P, 4, NH, B])
        slope = sb("slope", [P, NH, B])
        pk = sb("pk", [P, 4, NH, B])
        pacc = sb("pacc", [P, 4, NH, B])

        stage_g = sb("stage_g", [P, 2, NH, UW])
        stage_u = sb("stage_u", [P, 2, NH, UW])
        stage_d = sb("stage_d", [P, 2, UW // P, H])
        wg_hi = sb("wg_hi", [P, NH, HID], F16)
        wg_lo = sb("wg_lo", [P, NH, HID], F16)
        wu_hi = sb("wu_hi", [P, NH, HID], F16)
        wu_lo = sb("wu_lo", [P, NH, HID], F16)
        wd_hi = sb("wd_hi", [P, HID // P, H], F16)
        wd_lo = sb("wd_lo", [P, HID // P, H], F16)

        silu = sb("silu", [P, 2, GC])
        gu = sb("gu", [P, 2, GC])
        hid = sb("hid", [P, 2, GC])
        hid_hi = sb("hid_hi", [P, NG, GC], F16)
        hid_lo = sb("hid_lo", [P, NG, GC], F16)

        logit = sb("logit", [P, E + TOPK])
        top8 = sb("top8", [P, 8])
        half_max = sb("half_max", [P, 1])
        tz = sb("tz", [P, E])
        ez_den = sb("ez_den", [P, E])
        ez_rec = sb("ez_rec", [P, E])
        ez = sb("ez", [P, E])
        marked = sb("marked", [P, E + TOPK])
        ez_top = sb("ez_top", [P, E])
        ez_sum = sb("ez_sum", [P, 1])
        ez_inv = sb("ez_inv", [P, 1])
        comb = sb("comb", [P, E])
        comb16 = sb("comb16", [P, P], F16)
        combT = sb("combT", [P, P], F16)
        part = sb("part", [P, H])
        res = sb("res", [P, NC, H])

        ps_gate = [pb(f"ps_gate{i}", [P, GC]) for i in range(2)]
        ps_up = [pb(f"ps_up{i}", [P, GC]) for i in range(2)]
        ps_comb = pb("ps_comb", [P, GC])
        ps_out = pb("ps_out", [P, 2 * H])
        ps_scan = pb("ps_scan", [P, GC])
        ps_misc = pb("ps_misc", [P, GC])
        ps_logit = ps_misc[:, 0:E]
        ps_combT = ps_misc[:, P:P + P // 2].bitcast(F16)
        ps_coupled = ps_scan[:, 0:SW].rearrange("p (n b) -> p n b", n=NH)

        cond_in, bias_in, coup_in, router_in = sem("cond_in"), sem("bias_in"), sem("coup_in"), sem("router_in")
        x0_in, x_in = sem("x0_in"), sem("x_in")
        w_in = [[sem(f"w{kind}_in{u}") for kind in "gud"] for u in range(NU)]
        zeroed, ident_ok, consts_ok, sel_in = sem("zeroed"), sem("ident_ok"), sem("consts_ok"), sem("sel_in")
        coup_mm, coup_ok, cond_mm = sem("coup_mm"), sem("coup_ok"), sem("cond_mm")
        bias_ok, xT_mm, drive_ok = sem("bias_ok"), sem("xT_mm"), sem("drive_ok")
        drive_now_ok = sem("drive_now_ok")
        w_hi_ok, w_lo_ok = sem("w_hi_ok"), sem("w_lo_ok")
        y_ok, p_ok, th_ok, coupled = sem("y_ok"), sem("p_ok"), sem("th_ok"), sem("coupled")
        sq_ok, qd_ok, dq_ok, dsum_ok = sem("sq_ok"), sem("qd_ok"), sem("dq_ok"), sem("dsum_ok")
        slope_ok, cubic_ok, qdp_ok, base_ok, base3_ok, pacc_ok, raw_ok = (
            sem("slope_ok"), sem("cubic_ok"), sem("qdp_ok"), sem("base_ok"), sem("base3_ok"), sem("pacc_ok"),
            sem("raw_ok"))
        qhi_ok, qlo_ok, tok_ok = sem("qhi_ok"), sem("qlo_ok"), sem("tok_ok")
        gate_mm, up_mm, comb_mm, down_mm = sem("gate_mm"), sem("up_mm"), sem("comb_mm"), sem("down_mm")
        silu_ok, gu_ok, hid_ok, hhi_ok, hlo_ok = (
            sem("silu_ok"), sem("gu_ok"), sem("hid_ok"), sem("hhi_ok"), sem("hlo_ok"))
        logit_mm, logit_ok, half_ok, tz_ok = sem("logit_mm"), sem("logit_ok"), sem("half_ok"), sem("tz_ok")
        route_step, comb_hi_ok, comb_lo_ok = sem("route_step"), sem("comb_hi_ok"), sem("comb_lo_ok")
        combT_mm, combT_ok = sem("combT_mm"), sem("combT_ok")
        part_ok, res_ok, out_sent = sem("part_ok"), sem("res_ok"), sem("out_sent")

        def first(c):
            return isinstance(c, int) and c == 0

        def arg(s, k):
            return q_new[:, :, (s - 1) % SPC, :] if k == 0 else y[:, k - 1, :, :]

        def pieces_for(g):
            return 3 * NH * min(NU, ((g + 1) * GC - 1) // UW + 1)

        def weight_piece(u, kind, n):
            width = UW if u < NU - 1 else SI
            if kind < 2:
                cols = slice(u * UW, u * UW + width)
                hi, lo = ((wg_hi, wg_lo), (wu_hi, wu_lo))[kind]
                return (stage_g, stage_u)[kind][:, u % 2, n, 0:width], hi[:, n, cols], lo[:, n, cols]
            half = width // P // NH
            tiles = slice(u * UW // P + n * half, u * UW // P + (n + 1) * half)
            return stage_d[:, u % 2, n * half:(n + 1) * half, :], wd_hi[:, tiles, :], wd_lo[:, tiles, :]

        PIECES_0 = [[i - 1] if i >= 1 else [] for i in range(STG + 1)]
        PIECES_1 = [[STG + i] if STG + i < NCONV else [] for i in range(STG + 1)]
        NO_PIECES = [[]] * (STG + 1)

        def ps_xT(c, n):
            bank = (ps_gate[1], ps_up[0], ps_up[1], ps_comb)[c % 4]
            return bank[:, n * P:(n + 1) * P]

        def units_of(g):
            def tiles(kind, group):
                return [(kind, group, t) for t in range(GT)]
            down = tiles("down", (g - 2) % NG)
            if g == 0:
                return tiles("gate", g) + tiles("up", g) + down
            if g == 1:
                return tiles("gate", g) + [("comb", 0, 0)] + tiles("up", g) + [("comb", g, 0)] + down
            return tiles("gate", g) + tiles("up", g) + [("comb", g, 0)] + down

        UNITS = [u for g in range(NG) for u in units_of(g)]

        def slot_of(kind, g):
            last = max(i for i, u in enumerate(UNITS) if u[:2] == (kind, g))
            return last * STG // len(UNITS) + 1

        block = ctx.enter_context(nc.Block())

        @block.sync
        def _(sp):
            steps = x.rearrange("b (c s) h -> s b c h", s=SPC)
            sp.dma_start(cond_row[:, :], cond).then_inc(cond_in, 16)
            sp.dma_start(coup_row[:, :, :], coupling.rearrange("(n p) k -> p n k", p=P)).then_inc(coup_in, 16)
            sp.dma_start(bias_col[:, :], bias.rearrange("(n p) -> p n", p=P),
                         allow_slow_non_contiguous=True).then_inc(bias_in, 16)
            for s in range(SPC):
                sp.dma_start(x_tok[s * B:(s + 1) * B, 0, :], steps[s, :, 0, :]).then_inc(x0_in, 16)
            for u in range(NU):
                if u >= 2:
                    sp.wait_ge(w_hi_ok, 3 * NH * (u - 1))
                    sp.wait_ge(w_lo_ok, 3 * NH * (u - 1))
                routed = u < NU - 1
                for kind, (dst, w, ws) in enumerate(((stage_g, w_gate, ws_gate), (stage_u, w_up, ws_up))):
                    for n in range(NH):
                        if routed:
                            sp.dma_start(dst[:, u % 2, n, :].rearrange("p (e i) -> p e i", i=I),
                                         w[8 * u:8 * u + 8, n * P:(n + 1) * P, :].rearrange("e p i -> p e i"))\
                                .then_inc(w_in[u][kind], 16)
                        else:
                            sp.dma_start(dst[:, u % 2, n, 0:SI], ws[n * P:(n + 1) * P, :]).then_inc(w_in[u][kind], 16)
                wd = w_down.rearrange("e i h -> (e i) h")[u * UW:(u + 1) * UW, :] if routed else ws_down
                tiles = wd.shape[0] // P
                sp.dma_start(stage_d[:, u % 2, 0:tiles, :], wd.rearrange("(t p) h -> p t h", p=P))\
                    .then_inc(w_in[u][2], 16)
                if u == 0:
                    sp.dma_start(selector[:, :], unit_of).then_inc(sel_in, 16)
                    for s in range(SPC):
                        sp.dma_start(x_tok[s * B:(s + 1) * B, 1:NC, :], steps[s, :, 1:NC, :]).then_inc(x_in, 16)
                    sp.dma_start(router[:, :, :], router_w.rearrange("(n p) e -> p n e", p=P)).then_inc(router_in, 16)

            outs = out.rearrange("b (c s) h -> c s b h", s=SPC)
            for c in range(NC):
                sp.wait_ge(res_ok, c + 1)
                for s in range(SPC):
                    sp.dma_start(outs[c, s], res[s * B:(s + 1) * B, c, :]).then_inc(out_sent, 16)
            sp.wait_ge(out_sent, 16 * NC * SPC)

        @block.gpsimd
        def _(pool):
            nc.gpsimd.memset(identf[:, :], 0.0).then_inc(zeroed, 1)
            nc.gpsimd.memset(ident16[:, :], 0.0).then_inc(zeroed, 1)
            pool.wait_ge(zeroed, 2)
            for m in (identf, ident16):
                nc.gpsimd.affine_select(out=m[:, :], in_=m[:, :], compare_op=ALU.not_equal, fill=1.0, base=0,
                                        pattern=[[-1, P]], channel_multiplier=1).then_inc(ident_ok, 1)

            def sums(c, s, k):
                n, done = c * STG + 4 * s + k, c * SPC + s
                q, d = arg(s, 0), drive_now[:, :, s, :]
                pool.wait_ge(y_ok, n + 1)
                nc.gpsimd.tensor_tensor(sq[:, :, :], arg(s, k), arg(s, k), ALU.mult).then_inc(sq_ok, 1)
                if k == 0:
                    if s == 0:
                        pool.wait_ge(drive_now_ok, c + 1)
                    nc.gpsimd.tensor_tensor(qd_half[:, :, :], q, d, ALU.add).then_inc(qd_ok, 1)
                    pool.wait_ge(qd_ok, 2 * done + 1)
                    nc.gpsimd.tensor_tensor(qd_full[:, :, :], qd_half[:, :, :], d, ALU.add).then_inc(qd_ok, 1)
                    return
                nc.gpsimd.tensor_tensor(dq[:, k - 1, :, :], arg(s, k), q, ALU.subtract).then_inc(dq_ok, 1)
                pool.wait_ge(dq_ok, 3 * done + k)
                if k == 1:
                    nc.gpsimd.tensor_tensor(dsum[:, 0, :, :], dq[:, 0, :, :], d, ALU.add).then_inc(dsum_ok, 1)
                elif k == 2:
                    for i in range(2):
                        pool.wait_ge(dsum_ok, 4 * done + i + 1)
                        nc.gpsimd.tensor_tensor(dsum[:, i + 1, :, :], dsum[:, i, :, :], dq[:, 1, :, :], ALU.add)\
                            .then_inc(dsum_ok, 1)
                else:
                    pool.wait_ge(dsum_ok, 4 * done + 3)
                    nc.gpsimd.tensor_tensor(dsum[:, 3, :, :], dsum[:, 2, :, :], dq[:, 2, :, :], ALU.add)\
                        .then_inc(dsum_ok, 1)

            def q_low(c, s):
                n = c * SPC + s + 1
                pool.wait_ge(y_ok, 4 * n + 1)
                pool.wait_ge(qhi_ok, n)
                if s == 0 and not first(c):
                    pool.wait_ge(tok_ok, 2 * c)
                nc.gpsimd.tensor_tensor(q_lo[:, :, s, :], q_new[:, :, s, :], q_hi[:, :, s, :], ALU.subtract)\
                    .then_inc(qlo_ok, 1)

            def hidden_low(f, g):
                pool.wait_ge(hid_ok, NG * f + g + 1)
                pool.wait_ge(hhi_ok, NG * f + g + 1)
                if not first(f):
                    pool.wait_ge(down_mm, NG * (f - 1) + g + 1)
                nc.gpsimd.tensor_tensor(hid_lo[:, g, :], hid[:, g % 2, :], hid_hi[:, g, :], ALU.subtract)\
                    .then_inc(hlo_ok, 1)

            def chunk(c, scan, ffn):
                for i in range(STG + 1):
                    s, k = i // 4, i % 4
                    if scan and k == 0 and s > 0:
                        if i < STG:
                            sums(c, s, k)
                        q_low(c, s - 1)
                    elif scan:
                        sums(c, s, k)
                    for g in range(NG):
                        if ffn and slot_of("comb", g) == i:
                            hidden_low(c - 1, g)

            nc.gpsimd.memset(comb16[:, :], 0.0).then_inc(zeroed, 1)
            nc.gpsimd.memset(logit[:, :], LOW).then_inc(consts_ok, 1)
            pool.wait_ge(zeroed, 3)
            nc.gpsimd.memset(comb16[:, 2 * E:2 * E + 1], CSCALE).then_inc(consts_ok, 1)
            chunk(0, True, False)
            chunk(1, True, True)
            with pool.Fori(2, NC) as c:
                chunk(c, True, True)
            chunk(NC, False, True)

        @block.scalar
        def _(act):
            act.wait_ge(bias_in, 16)
            nc.scalar.activation(bias_dt[:, :], bias_col[:, :], ACT.Copy, scale=DT / 2, bias=-PSHIFT * DT / 2)\
                .then_inc(bias_ok, 1)
            act.wait_ge(bias_ok, 1)

            def drive_of(c):
                act.wait_ge(xT_mm, c + 1)
                for n in range(NH):
                    nc.scalar.activation(drive[:, c, n, :, :], ps_xT(c, n).rearrange("p (s b) -> p s b", b=B),
                                         ACT.Identity, scale=DT / 2, bias=bias_dt[:, n:n + 1]).then_inc(drive_ok, 1)

            def tanh(c, s, k):
                act.wait_ge(y_ok, c * STG + 4 * s + k + 1)
                nc.scalar.activation(th[:, :, :], arg(s, k), ACT.Tanh).then_inc(th_ok, 1)

            def q_high(c, s):
                act.wait_ge(y_ok, 4 * (c * SPC + s + 1) + 1)
                if s == 0 and not first(c):
                    act.wait_ge(tok_ok, 2 * c)
                nc.scalar.activation(q_hi[:, :, s, :], q_new[:, :, s, :], ACT.Copy).then_inc(qhi_ok, 1)

            def split_high(piece):
                u, kind, n = piece // (3 * NH), piece // NH % 3, piece % NH
                if n == 0:
                    act.wait_ge(w_in[u][kind], 16 if kind == 2 else 16 * NH)
                src, hi, _ = weight_piece(u, kind, n)
                nc.scalar.activation(hi, src, ACT.Copy, scale=WSCALE).then_inc(w_hi_ok, 1)

            def silu_of(f, g):
                act.wait_ge(gate_mm, NG * f + g + 1)
                if g >= 2:
                    act.wait_ge(gu_ok, NG * f + g - 1)
                elif not first(f):
                    act.wait_ge(gu_ok, NG * f)
                nc.scalar.activation(silu[:, g % 2, :], ps_gate[g % 2][:, :], ACT.Silu, scale=1 / WSCALE)\
                    .then_inc(silu_ok, 1)

            def hidden_high(f, g):
                act.wait_ge(hid_ok, NG * f + g + 1)
                if not first(f):
                    act.wait_ge(down_mm, NG * (f - 1) + g + 1)
                nc.scalar.activation(hid_hi[:, g, :], hid[:, g % 2, :], ACT.Copy).then_inc(hhi_ok, 1)

            def route_tanh(f):
                act.wait_ge(half_ok, f + 1)
                nc.scalar.activation(tz[:, :], logit[:, 0:E], ACT.Tanh, scale=0.5, bias=half_max[:, 0:1])\
                    .then_inc(tz_ok, 1)

            def chunk(c, scan, ffn, pieces):
                for i in range(STG + 1):
                    s, k = i // 4, i % 4
                    if scan and i < STG:
                        tanh(c, s, k)
                    if scan and k == 0 and s > 0:
                        q_high(c, s - 1)
                    if ffn and i == 1:
                        route_tanh(c - 1)
                    for piece in pieces[i]:
                        split_high(piece)
                    if scan and not ffn and i % 2 == 0 and i // 2 + 1 < NC:
                        drive_of(i // 2 + 1)
                    for g in range(NG):
                        if ffn and slot_of("gate", g) == i:
                            silu_of(c - 1, g)
                        if ffn and slot_of("comb", g) == i:
                            hidden_high(c - 1, g)

            drive_of(0)
            chunk(0, True, False, PIECES_0)
            chunk(1, True, True, PIECES_1)
            with act.Fori(2, NC) as c:
                chunk(c, True, True, NO_PIECES)
            chunk(NC, False, True, NO_PIECES)

        @block.vector
        def _(dve):
            stt, tt, ts = nc.vector.scalar_tensor_tensor, nc.vector.tensor_tensor, nc.vector.tensor_scalar

            dve.wait_ge(coup_mm, 1)
            nc.vector.tensor_copy(coupT[:, :, :], ps_gate[0][:, :].rearrange("p (n m) -> p n m", n=NH))\
                .then_inc(coup_ok, 1)
            dve.wait_ge(cond_mm, 1)
            c0 = ps_coupled
            nc.vector.tensor_copy(q_new[:, :, SPC - 1, :], c0).then_inc(y_ok, 1)
            ts(pk[:, 0, :, :], c0, -PSHIFT, None, ALU.add).then_inc(p_ok, 1)

            def before_coupling(c, s, k):
                n, done = c * STG + 4 * s + k, c * SPC + s
                yk, q = arg(s, k), arg(s, 0)
                dve.wait_ge(y_ok, n + 1)
                dve.wait_ge(p_ok, n + 1)
                stt(out=slope[:, :, :], in0=pk[:, k, :, :], scalar=-BETA, in1=yk, op0=ALU.mult, op1=ALU.add)\
                    .then_inc(slope_ok, 1)
                dve.wait_ge(sq_ok, n + 1)
                stt(out=cubic[:, :, :], in0=sq[:, :, :], scalar=-3.0, in1=yk, op0=ALU.add, op1=ALU.mult)\
                    .then_inc(cubic_ok, 1)
                if k < 3:
                    dve.wait_ge(qd_ok, 2 * done + (1 if k < 2 else 2))
                qd = (qd_half, qd_half, qd_full)[k][:, :, :] if k < 3 else q
                stt(out=qdp[:, :, :], in0=pk[:, k, :, :], scalar=-CQ[k], in1=qd, op0=ALU.mult, op1=ALU.add)\
                    .then_inc(qdp_ok, 1)
                dve.wait_ge(slope_ok, n + 1)
                if k < 3:
                    stt(out=pk[:, k + 1, :, :], in0=slope[:, :, :], scalar=CP[k], in1=pk[:, 0, :, :],
                        op0=ALU.mult, op1=ALU.add).then_inc(p_ok, 1)
                if k > 0:
                    dve.wait_ge(pacc_ok, 4 * done + k)
                stt(out=pacc[:, k, :, :], in0=slope[:, :, :], scalar=CPSUM[k],
                    in1=pacc[:, k - 1, :, :] if k > 0 else pk[:, 0, :, :],
                    op0=ALU.mult, op1=ALU.add).then_inc(pacc_ok, 1)
                dve.wait_ge(cubic_ok, n + 1)
                dve.wait_ge(qdp_ok, n + 1)
                stt(out=base[:, :, :], in0=cubic[:, :, :], scalar=-CQ[k] / 3, in1=qdp[:, :, :],
                    op0=ALU.mult, op1=ALU.add).then_inc(base_ok, 1)
                dve.wait_ge(base_ok, n + 1)
                if k == 3:
                    dve.wait_ge(dsum_ok, 4 * (done + 1))
                    stt(out=base3[:, :, :], in0=dsum[:, 3, :, :], scalar=1 / 3, in1=base[:, :, :],
                        op0=ALU.mult, op1=ALU.add).then_inc(base3_ok, 1)
                    dve.wait_ge(pacc_ok, 4 * (done + 1))
                    ts(pk[:, 0, :, :], pacc[:, 3, :, :], CLAMP - PSHIFT, -CLAMP - PSHIFT, ALU.min, ALU.max)\
                        .then_inc(p_ok, 1)
                    dve.wait_ge(base3_ok, done + 1)

            def after_coupling(c, s, k):
                n, done = c * STG + 4 * s + k, c * SPC + s
                dve.wait_ge(coupled, n + 1)
                if k < 3:
                    stt(out=y[:, k, :, :], in0=ps_coupled, scalar=CQ[k], in1=base[:, :, :],
                        op0=ALU.mult, op1=ALU.add).then_inc(y_ok, 1)
                    return
                stt(out=q_raw[:, :, :], in0=ps_coupled, scalar=CQ[3], in1=base3[:, :, :],
                    op0=ALU.mult, op1=ALU.add).then_inc(raw_ok, 1)
                dve.wait_ge(raw_ok, done + 1)
                if s == 0 and not first(c):
                    dve.wait_ge(logit_mm, c)
                ts(q_new[:, :, s, :], q_raw[:, :, :], CLAMP, -CLAMP, ALU.min, ALU.max).then_inc(y_ok, 1)

            def copy_chunk(c):
                if not first(c):
                    dve.wait_ge(up_mm, NG * c)
                dve.wait_ge(qhi_ok, SPC * (c + 1))
                nc.vector.tensor_copy(tok_hi[:, :, :], q_hi[:, :, :, :].rearrange("p n s b -> p n (s b)"))\
                    .then_inc(tok_ok, 1)
                dve.wait_ge(qlo_ok, SPC * (c + 1))
                nc.vector.tensor_copy(tok_lo[:, :, :], q_lo[:, :, :, :].rearrange("p n s b -> p n (s b)"))\
                    .then_inc(tok_ok, 1)

            def split_low(piece):
                u, kind, n = piece // (3 * NH), piece // NH % 3, piece % NH
                dve.wait_ge(w_hi_ok, piece + 1)
                src, hi, lo = weight_piece(u, kind, n)
                stt(out=lo, in0=src, scalar=WSCALE, in1=hi, op0=ALU.mult, op1=ALU.subtract).then_inc(w_lo_ok, 1)

            LINKS = 10

            def route_pick(f):
                r = LINKS * f
                dve.wait_ge(logit_mm, f + 1)
                if first(f):
                    dve.wait_ge(consts_ok, 2)
                nc.vector.tensor_copy(logit[:, 0:E], ps_logit).then_inc(route_step, 1)
                nc.vector.max(out=top8[:, :], in_=ps_logit).then_inc(route_step, 1)
                dve.wait_ge(route_step, r + 2)
                nc.vector.memset(top8[:, TOPK:8], LOW).then_inc(route_step, 1)
                dve.wait_ge(route_step, r + 3)
                ts(half_max[:, :], top8[:, 0:1], -0.5, None, ALU.mult).then_inc(half_ok, 1)
                nc.vector.match_replace(out=marked[:, :], in_to_replace=top8[:, :], in_values=logit[:, :],
                                        imm_value=HIGH).then_inc(route_step, 1)

            def route_weights(f):
                r = LINKS * f
                dve.wait_ge(tz_ok, f + 1)
                ts(ez_den[:, :], tz[:, :], -1.0, 1.0, ALU.mult, ALU.add).then_inc(route_step, 1)
                dve.wait_ge(route_step, r + 5)
                nc.vector.reciprocal(ez_rec[:, :], ez_den[:, :]).then_inc(route_step, 1)
                dve.wait_ge(route_step, r + 6)
                stt(out=ez[:, :], in0=tz[:, :], scalar=1.0, in1=ez_rec[:, :], op0=ALU.add, op1=ALU.mult)\
                    .then_inc(route_step, 1)
                dve.wait_ge(route_step, r + 7)
                stt(out=ez_top[:, :], in0=marked[:, 0:E], scalar=HIGH, in1=ez[:, :], op0=ALU.is_ge, op1=ALU.mult,
                    accum_out=ez_sum[:, :]).then_inc(route_step, 1)
                dve.wait_ge(route_step, r + 8)
                nc.vector.reciprocal(ez_inv[:, :], ez_sum[:, :]).then_inc(route_step, 1)
                dve.wait_ge(route_step, r + 9)
                ts(comb[:, :], ez_top[:, :], ez_inv[:, 0:1], CSCALE, ALU.mult, ALU.mult).then_inc(route_step, 1)

            def route_split(f):
                dve.wait_ge(route_step, LINKS * (f + 1))
                if not first(f):
                    dve.wait_ge(combT_mm, f)
                nc.vector.tensor_copy(comb16[:, 0:E], comb[:, :]).then_inc(comb_hi_ok, 1)
                dve.wait_ge(comb_hi_ok, f + 1)
                tt(comb16[:, E:2 * E], comb[:, :], comb16[:, 0:E], ALU.subtract).then_inc(comb_lo_ok, 1)

            def route_transposed(f):
                dve.wait_ge(combT_mm, f + 1)
                if not first(f):
                    dve.wait_ge(comb_mm, NG * f)
                nc.vector.tensor_copy(combT[:, :], ps_combT).then_inc(combT_ok, 1)

            def gate_times_up(f, g):
                dve.wait_ge(silu_ok, NG * f + g + 1)
                dve.wait_ge(up_mm, NG * f + g + 1)
                tt(gu[:, g % 2, :], ps_up[g % 2][:, :], silu[:, g % 2, :], ALU.mult).then_inc(gu_ok, 1)

            def times_routing(f, g):
                dve.wait_ge(gu_ok, NG * f + g + 1)
                dve.wait_ge(comb_mm, NG * f + g + 1)
                if g >= 2:
                    dve.wait_ge(hlo_ok, NG * f + g - 1)
                elif not first(f):
                    dve.wait_ge(hlo_ok, NG * f)
                stt(out=hid[:, g % 2, :], in0=ps_comb[:, :], scalar=HSCALE, in1=gu[:, g % 2, :],
                    op0=ALU.mult, op1=ALU.mult).then_inc(hid_ok, 1)

            def finish(f):
                dve.wait_ge(down_mm, NG * (f + 1))
                if first(f):
                    dve.wait_ge(x0_in, 16 * SPC)
                    dve.wait_ge(x_in, 16 * SPC)
                tt(part[:, :], ps_out[:, H:2 * H], x_tok[:, f, :], ALU.add).then_inc(part_ok, 1)
                dve.wait_ge(part_ok, f + 1)
                tt(res[:, f, :], ps_out[:, 0:H], part[:, :], ALU.add).then_inc(res_ok, 1)

            def chunk(c, scan, ffn, pieces, finish_before=True):
                if scan:
                    if isinstance(c, int):
                        dve.wait_ge(drive_ok, NH * (1 if c == 0 else NC))
                    if not first(c):
                        dve.wait_ge(dsum_ok, 4 * SPC * c)
                    nc.vector.tensor_copy(drive_now[:, :, :, :], drive[:, c, :, :, :]).then_inc(drive_now_ok, 1)
                for i in range(STG + 1):
                    s, k = i // 4, i % 4
                    if scan and i < STG:
                        before_coupling(c, s, k)
                    for piece in pieces[i]:
                        split_low(piece)
                    for g in range(NG):
                        if ffn and slot_of("up", g) == i:
                            gate_times_up(c - 1, g)
                        if ffn and slot_of("comb", g) == i:
                            times_routing(c - 1, g)
                    if ffn and finish_before and i == slot_of("down", NG - 1):
                        finish(c - 2)
                    if scan and i < STG:
                        after_coupling(c, s, k)
                    if ffn and i == 0:
                        route_pick(c - 1)
                    if ffn and i == 1:
                        route_weights(c - 1)
                        route_split(c - 1)
                    if ffn and i == 2:
                        route_transposed(c - 1)
                if scan:
                    copy_chunk(c)

            chunk(0, True, False, PIECES_0)
            chunk(1, True, True, PIECES_1, finish_before=False)
            with dve.Fori(2, NC) as c:
                chunk(c, True, True, NO_PIECES)
            chunk(NC, False, True, NO_PIECES)
            finish(NC - 1)

        @block.tensor
        def _(pe):
            mm = nc.tensor.matmul

            def x_transposed(c):
                if c == 0:
                    pe.wait_ge(x0_in, 16 * SPC)
                elif c == 1:
                    pe.wait_ge(x_in, 16 * SPC)
                if c >= 4:
                    pe.wait_ge(drive_ok, NH * (c - 3))
                for n in range(NH):
                    last = nc.tensor.transpose(ps_xT(c, n), x_tok[:, c, n * P:(n + 1) * P], identf[:, :])
                last.then_inc(xT_mm, 1)

            def couple(c, s, k):
                pe.wait_ge(th_ok, c * STG + 4 * s + k + 1)
                for m in range(NH):
                    for n in range(NH):
                        last = mm(ps_scan[:, m * B:(m + 1) * B], coupT[:, n, m * P:(m + 1) * P], th[:, n, :],
                                  start=(n == 0), stop=(n == NH - 1))
                last.then_inc(coupled, 1)

            def project(ps, hi, lo, col, t):
                for n in range(NH):
                    w_hi, w_lo = hi[:, n, col:col + P], lo[:, n, col:col + P]
                    out_t = ps[:, t * P:(t + 1) * P]
                    mm(out_t, w_hi, tok_hi[:, n, :], start=(n == 0), stop=False)
                    mm(out_t, w_hi, tok_lo[:, n, :], start=False, stop=False)
                    last = mm(out_t, w_lo, tok_hi[:, n, :], start=False, stop=(n == NH - 1))
                return last

            def unit(f, kind, g, t, weights_new):
                n, col = NG * f + g, g * GC + t * P
                if kind == "gate":
                    if t == 0:
                        if g == 0:
                            pe.wait_ge(tok_ok, 2 * (f + 1))
                        if weights_new:
                            pe.wait_ge(w_lo_ok, pieces_for(g))
                        if g >= 2:
                            pe.wait_ge(silu_ok, n - 1)
                        elif g == 0 and not first(f):
                            pe.wait_ge(silu_ok, n)
                    last = project(ps_gate[g % 2], wg_hi, wg_lo, col, t)
                    if t == GT - 1:
                        last.then_inc(gate_mm, 1)
                elif kind == "up":
                    if t == 0:
                        if g >= 2:
                            pe.wait_ge(gu_ok, n - 1)
                        elif g == 0 and not first(f):
                            pe.wait_ge(gu_ok, n)
                    last = project(ps_up[g % 2], wu_hi, wu_lo, col, t)
                    if t == GT - 1:
                        last.then_inc(up_mm, 1)
                elif kind == "comb":
                    if g == 0:
                        pe.wait_ge(combT_ok, f + 1)
                    if g > 0 or not first(f):
                        pe.wait_ge(hid_ok, n)
                    for t in range(GT):
                        last = mm(ps_comb[:, t * P:(t + 1) * P], selector[:, col + t * P:col + (t + 1) * P],
                                  combT[:, :], start=True, stop=True)
                    last.then_inc(comb_mm, 1)
                else:
                    if t == 0:
                        pe.wait_ge(hlo_ok, n + 1)
                        if g == 0 and not first(f):
                            pe.wait_ge(res_ok, f)
                    cross = dict(start=False, stop=(g == NG - 1 and t == GT - 1))
                    tile = g * GT + t
                    h_hi, h_lo = hid_hi[:, g, t * P:(t + 1) * P], hid_lo[:, g, t * P:(t + 1) * P]
                    mm(ps_out[:, 0:H], h_hi, wd_hi[:, tile, :], start=(g == 0 and t == 0), **{"stop": cross["stop"]},
                       skip_group_check=True)
                    mm(ps_out[:, H:2 * H], h_hi, wd_lo[:, tile, :], skip_group_check=True, **cross)
                    last = mm(ps_out[:, H:2 * H], h_lo, wd_hi[:, tile, :], skip_group_check=True, **cross)
                    if t == GT - 1:
                        last.then_inc(down_mm, 1)

            def logits(f):
                for n in range(NH):
                    last = mm(ps_logit, q_new[:, n, :, :].rearrange("p s b -> p (s b)"), router[:, n, :],
                              start=(n == 0), stop=(n == NH - 1))
                last.then_inc(logit_mm, 1)

            def route_transpose(f):
                pe.wait_ge(comb_lo_ok, f + 1)
                nc.tensor.transpose(ps_combT, comb16[:, :], ident16[:, :]).then_inc(combT_mm, 1)

            def chunk(c, scan, ffn, weights_new=False, down_before=True):
                if ffn:
                    if weights_new:
                        pe.wait_ge(router_in, 16)
                        pe.wait_ge(sel_in, 16)
                        pe.wait_ge(drive_ok, NH * NC)
                    pe.wait_ge(y_ok, c * STG + 1)
                    logits(c - 1)
                for i in range(STG):
                    s, k = i // 4, i % 4
                    if scan:
                        couple(c, s, k)
                    if ffn and i == 2:
                        route_transpose(c - 1)
                    if scan and not ffn and i % 2 == 0 and i // 2 + 1 < NC:
                        x_transposed(i // 2 + 1)
                    if ffn:
                        for j, (kind, g, t) in enumerate(UNITS):
                            if j * STG // len(UNITS) == i:
                                if kind == "down" and j < 2 * len(UNITS) // NG:
                                    if down_before:
                                        unit(c - 2, kind, g, t, False)
                                else:
                                    unit(c - 1, kind, g, t, weights_new)

            pe.wait_ge(ident_ok, 2)
            pe.wait_ge(coup_in, 16)
            for n in range(NH):
                for m in range(NH):
                    last = nc.tensor.transpose(ps_gate[0][:, n * H + m * P:n * H + (m + 1) * P],
                                               coup_row[:, m, n * P:(n + 1) * P], identf[:, :])
            last.then_inc(coup_mm, 1)
            pe.wait_ge(cond_in, 16)
            for n in range(NH):
                last = nc.tensor.transpose(ps_scan[:, n * B:(n + 1) * B], cond_row[:, n * P:(n + 1) * P],
                                           identf[0:B, 0:B])
            last.then_inc(cond_mm, 1)
            x_transposed(0)
            pe.wait_ge(coup_ok, 1)
            pe.wait_ge(p_ok, 1)

            chunk(0, True, False)
            chunk(1, True, True, weights_new=True, down_before=False)
            with pe.Fori(2, NC) as c:
                chunk(c, True, True)
            chunk(NC, False, True)
            for g in (NG - 2, NG - 1):
                for t in range(GT):
                    unit(NC - 1, "down", g, t, False)


_INS = ["x", "cond_2048", "L0_cond_coupling", "L0_cond_bias", "L0_ffn_router_w", "L0_ffn_w_gate", "L0_ffn_w_up",
        "L0_ffn_w_down", "L0_ffn_ws_gate", "L0_ffn_ws_up", "L0_ffn_ws_down"]
_OUTS = [((B, T, H), "float32")]


def kernel(**inputs):
    import numpy as _np
    import concourse.bacc as _bacc
    from concourse import mybir as _mybir
    from concourse.bass_utils import run_bass_kernel_spmd as _run

    nc = _bacc.Bacc("TRN2", target_bir_lowering=False, num_devices=1)
    arrays, args = {}, []
    for name in _INS:
        a = _np.ascontiguousarray(inputs[name])
        arrays[f"in_{name}_dram"] = a
        args.append(nc.dram_tensor(f"in_{name}_dram", a.shape, _mybir.dt.from_np(a.dtype), kind="ExternalInput").ap())
    unit_of = _np.zeros((P, HID), _np.float16)
    for e in range(E):
        unit_of[[e, E + e], e * I:(e + 1) * I] = 1
    unit_of[2 * E, E * I:] = 1
    arrays["unit_of_dram"] = unit_of
    args.append(nc.dram_tensor("unit_of_dram", unit_of.shape, F16, kind="ExternalInput").ap())
    for i, (shape, dtype) in enumerate(_OUTS):
        dt = _mybir.dt.from_np(_np.dtype(dtype))
        args.append(nc.dram_tensor(f"out_{i}_dram", shape, dt, kind="ExternalOutput").ap())
    build(nc, *args)
    r = _run(nc, [arrays], core_ids=[0])
    return r.results[0]["out_0_dram"]
```

```python
import concourse.bass as bass
from concourse import mybir
from contextlib import ExitStack

F32 = mybir.dt.float32
F16 = mybir.dt.float16
ALU = mybir.AluOpType
ACT = mybir.ActivationFunctionType

P = 128
B, T, H = 32, 32, 256
E, I, SI, TOPK = 32, 96, 512, 4
NH = H // P
SPC = P // B
NC = T // SPC
SW = NH * B
GT = 4
GC = GT * P
NG = (E * I + SI) // GC
NGR = E * I // GC
UW = 8 * I
NU = E // 8 + 1
NCONV = 3 * NH * NU
HID = NG * GC
STG = 4 * SPC

DT, EPS, ALPHA, BETA, CLAMP = 0.01, 0.08, 0.7, 0.8, 20.0
CQ = [DT / 2, DT / 2, DT, DT / 6]
CP = [v * EPS for v in CQ]
CPSUM = [DT / 6 * EPS * w for w in (1, 2, 2, 1)]
PSHIFT = ALPHA / BETA

WSCALE = 16.0
CSCALE = 1.0 / WSCALE / 16.0
LOW = -1.0e30
HIGH = 1.0e30


def build(nc, x, cond, coupling, bias, router_w, w_gate, w_up, w_down, ws_gate, ws_up, ws_down, out):
    ctx = ExitStack()
    with ctx:
        def sb(name, shape, dt=F32):
            return ctx.enter_context(nc.sbuf_tensor(name, shape, dt))

        def pb(name, shape, dt=F32):
            return ctx.enter_context(nc.psum_tensor(name, shape, dt))

        def sem(name):
            return ctx.enter_context(nc.semaphore(name))

        x_tok = sb("x_tok", [P, NC, H])
        drive = sb("drive", [P, NC, NH, SPC, B])
        drive_now = sb("drive_now", [P, NH, SPC, B])
        bias_row = sb("bias_row", [NH, P])
        bias_dt = sb("bias_dt", [P, NH])
        cond_row = sb("cond_row", [B, H])
        coup_row = sb("coup_row", [P, NH, H])
        coup_hi = sb("coup_hi", [P, NH, H], F16)
        coup_lo = sb("coup_lo", [P, NH, H], F16)
        router = sb("router", [P, NH, E])
        identf = sb("identf", [P, P])
        ident16 = sb("ident16", [P, P], F16)

        q_new = sb("q_new", [P, NH, SPC, B])
        q_raw = sb("q_raw", [P, NH, B])
        q_hi = sb("q_hi", [P, NH, SPC, B], F16)
        q_lo = sb("q_lo", [P, NH, SPC, B], F16)
        tok_hi = sb("tok_hi", [P, NH, SPC * B], F16)
        tok_lo = sb("tok_lo", [P, NH, SPC * B], F16)
        y = sb("y", [P, 3, NH, B])
        th = sb("th", [P, NH, B])
        th_hi = sb("th_hi", [P, NH, B], F16)
        th_lo = sb("th_lo", [P, NH, B], F16)
        sq = sb("sq", [P, NH, B])
        cubic = sb("cubic", [P, NH, B])
        base = sb("base", [P, NH, B])
        base3 = sb("base3", [P, NH, B])
        qdp = sb("qdp", [P, 4, NH, B])
        qd_half = sb("qd_half", [P, NH, B])
        qd_full = sb("qd_full", [P, NH, B])
        dq = sb("dq", [P, 3, NH, B])
        dsum = sb("dsum", [P, 4, NH, B])
        slope = sb("slope", [P, NH, B])
        pk = sb("pk", [P, 4, NH, B])
        pacc = sb("pacc", [P, 4, NH, B])

        stage_g = sb("stage_g", [P, 2, NH, UW])
        stage_u = sb("stage_u", [P, 2, NH, UW])
        stage_d = sb("stage_d", [P, 2, UW // P, H])
        wg_hi = sb("wg_hi", [P, NH, HID], F16)
        wg_lo = sb("wg_lo", [P, NH, HID], F16)
        wu_hi = sb("wu_hi", [P, NH, HID], F16)
        wu_lo = sb("wu_lo", [P, NH, HID], F16)
        wd = sb("wd", [P, HID // P, 2, H], F16)

        silu = sb("silu", [P, 2, GC])
        hid = sb("hid", [P, NG, GC])
        hid_hi = sb("hid_hi", [P, NG, GC], F16)
        hid_lo = sb("hid_lo", [P, NG, GC], F16)
        hidT = sb("hidT", [P, NG, 2 * GT, P], F16)

        logit = sb("logit", [P, E + TOPK])
        top8 = sb("top8", [P, 8])
        half_max = sb("half_max", [P, 1])
        tz = sb("tz", [P, E])
        ez_den = sb("ez_den", [P, E])
        ez_rec = sb("ez_rec", [P, E])
        ez = sb("ez", [P, E])
        marked = sb("marked", [P, E + TOPK])
        ez_top = sb("ez_top", [P, E])
        ez_sum = sb("ez_sum", [P, 1])
        ez_inv = sb("ez_inv", [P, 1])
        comb = sb("comb", [P, E])
        part = sb("part", [P, H])

        ps_gate = [pb(f"ps_gate{i}", [P, GC]) for i in range(2)]
        ps_up = [pb(f"ps_up{i}", [P, GC]) for i in range(2)]
        ps_hidT = pb("ps_hidT", [P, 2 * GT, P], F16)
        ps_out = pb("ps_out", [P, 2 * H])
        ps_scan = pb("ps_scan", [P, GC])
        ps_misc = pb("ps_misc", [P, GC])
        ps_logit = ps_misc[:, 0:E]
        ps_coupled = ps_scan[:, 0:SW].rearrange("p (n b) -> p n b", n=NH)

        cond_in, bias_in, coup_in, router_in = sem("cond_in"), sem("bias_in"), sem("coup_in"), sem("router_in")
        x0_in, x_in = sem("x0_in"), sem("x_in")
        w_in = [[sem(f"w{kind}_in{u}") for kind in "gud"] for u in range(NU)]
        zeroed, ident_ok, consts_ok = sem("zeroed"), sem("ident_ok"), sem("consts_ok")
        coup_mm, coup_hi_ok, coup_lo_ok, cond_mm, bias_mm = (
            sem("coup_mm"), sem("coup_hi_ok"), sem("coup_lo_ok"), sem("cond_mm"), sem("bias_mm"))
        bias_ok, xT_mm, drive_ok = sem("bias_ok"), sem("xT_mm"), sem("drive_ok")
        drive_now_ok = sem("drive_now_ok")
        w_hi_ok, w_lo_ok = sem("w_hi_ok"), sem("w_lo_ok")
        y_ok, p_ok, coupled = sem("y_ok"), sem("p_ok"), sem("coupled")
        th_hi_ok, th_ok, th_lo_ok = sem("th_hi_ok"), sem("th_ok"), sem("th_lo_ok")
        sq_ok, qd_ok, dq_ok, dsum_ok = sem("sq_ok"), sem("qd_ok"), sem("dq_ok"), sem("dsum_ok")
        qdp_pool, qdp_ok = sem("qdp_pool"), sem("qdp_ok")
        slope_ok, cubic_ok, base_ok, base3_ok, pacc_ok, raw_ok = (
            sem("slope_ok"), sem("cubic_ok"), sem("base_ok"), sem("base3_ok"), sem("pacc_ok"),
            sem("raw_ok"))
        qhi_ok, qlo_ok, tok_ok = sem("qhi_ok"), sem("qlo_ok"), sem("tok_ok")
        gate_mm, up_mm, hidT_mm, down_mm = sem("gate_mm"), sem("up_mm"), sem("hidT_mm"), sem("down_mm")
        silu_ok, hid_ok, hhi_ok, hlo_ok, hidT_ok = (
            sem("silu_ok"), sem("hid_ok"), sem("hhi_ok"), sem("hlo_ok"), sem("hidT_ok"))
        logit_mm, logit_ok, half_ok, tz_ok = sem("logit_mm"), sem("logit_ok"), sem("half_ok"), sem("tz_ok")
        route_step = sem("route_step")
        part_ok, res_ok, out_sent = sem("part_ok"), sem("res_ok"), sem("out_sent")

        def first(c):
            return isinstance(c, int) and c == 0

        def arg(s, k):
            return q_new[:, :, (s - 1) % SPC, :] if k == 0 else y[:, k - 1, :, :]

        def pieces_for(g):
            return 3 * NH * min(NU, ((g + 1) * GC - 1) // UW + 1)

        def weight_piece(u, kind, n):
            width = UW if u < NU - 1 else SI
            if kind < 2:
                cols = slice(u * UW, u * UW + width)
                hi, lo = ((wg_hi, wg_lo), (wu_hi, wu_lo))[kind]
                return (stage_g, stage_u)[kind][:, u % 2, n, 0:width], hi[:, n, cols], lo[:, n, cols]
            half = width // P // NH
            tiles = slice(u * UW // P + n * half, u * UW // P + (n + 1) * half)
            return stage_d[:, u % 2, n * half:(n + 1) * half, :], wd[:, tiles, 0, :], wd[:, tiles, 1, :]

        PIECES_0 = [[i] for i in range(STG)]
        PIECES_1 = [[STG + i] if STG + i < NCONV else [] for i in range(STG)]
        NO_PIECES = [[]] * STG

        def ps_xT(c, n):
            bank = (ps_gate[1], ps_up[0], ps_up[1], ps_out)[c % 4]
            return bank[:, n * P:(n + 1) * P]

        TURN_LAG, DOWN_LAG = 3, 5
        BLOCK = 3 * H * GT + 2 * 3 * NH * GC + 2 * GT * P

        def slot_at(b, columns):
            return (b * BLOCK + columns) * STG // (NG * BLOCK)

        MATRIX = [[] for _ in range(2 * STG)]
        for b in range(NG + DOWN_LAG):
            cols = 0
            for i in range(GT):
                if b >= DOWN_LAG:
                    MATRIX[slot_at(b, cols)].append(("down", b - DOWN_LAG, i))
                cols += 3 * H
            for i in range(3 * NH):
                if b < NG:
                    MATRIX[slot_at(b, cols)].append(("gate", b, i))
                cols += GC
            if TURN_LAG <= b < NG + TURN_LAG:
                MATRIX[slot_at(b, cols)].append(("turn", b - TURN_LAG, 0))
            cols += 2 * GT * P
            for i in range(3 * NH):
                if b < NG:
                    MATRIX[slot_at(b, cols)].append(("up", b, i))
                cols += GC

        def after(kind, g):
            return max(i for i, units in enumerate(MATRIX) if any(u[:2] == (kind, g) for u in units)) + 1

        def segments(g):
            out, unit, end = [], g * GC, (g + 1) * GC
            while unit < end:
                e = unit // I
                stop = min(end, (e + 1) * I if e < E else unit + GC // 4)
                out.append((e if e < E else None, unit - g * GC, stop - g * GC))
                unit = stop
            return out

        VECTOR, SCALAR = ([[] for _ in range(2 * STG)] for _ in range(2))
        vector_load, scalar_load = [0] * STG, [0] * STG
        vector_load[1] = vector_load[2] = 400
        VECTOR_ROOM, SCALAR_ROOM = 1180, 1060

        def place(table, load, room, item, columns, slot):
            while load[slot % STG] + columns > room:
                slot += 1
            load[slot % STG] += columns
            table[slot].append(item)
            return slot

        at = after("down", NG - 1)
        for j in range(2):
            at = place(VECTOR, vector_load, VECTOR_ROOM, ("finish", 0, j), H + 60, at)
        for g in range(NG):
            at = place(SCALAR, scalar_load, SCALAR_ROOM, ("silu", g, 0), GC, after("gate", g))
            at = max(at, after("up", g))
            for j, (_, a, b) in enumerate(segments(g)):
                at = place(VECTOR, vector_load, VECTOR_ROOM, ("product", g, j), b - a + 100, at)
            at = place(SCALAR, scalar_load, SCALAR_ROOM, ("high", g, 0), GC, at + 1)
            for j in range(2):
                at = place(VECTOR, vector_load, VECTOR_ROOM, ("low", g, j), GC // 2 + 60, at + 1 - j)
            assert at < min(i for i, u in enumerate(MATRIX) if ("turn", g, 0) in u) + 1, (g, at)
            at = after("turn", g)
            for j in range(2):
                at = place(SCALAR, scalar_load, SCALAR_ROOM, ("turned", g, j), GC, at)

        block = ctx.enter_context(nc.Block())

        @block.sync
        def _(sp):
            steps = x.rearrange("b (c s) h -> s b c h", s=SPC)
            sp.dma_start(cond_row[:, :], cond).then_inc(cond_in, 16)
            sp.dma_start(coup_row[:, :, :], coupling.rearrange("(n p) k -> p n k", p=P)).then_inc(coup_in, 16)
            sp.dma_start(bias_row[:, :], bias.rearrange("(n p) -> n p", p=P)).then_inc(bias_in, 16)
            for s in range(SPC):
                sp.dma_start(x_tok[s * B:(s + 1) * B, 0, :], steps[s, :, 0, :]).then_inc(x0_in, 16)
            for u in range(NU):
                if u >= 2:
                    sp.wait_ge(w_hi_ok, 3 * NH * (u - 1))
                    sp.wait_ge(w_lo_ok, 3 * NH * (u - 1))
                routed = u < NU - 1
                for kind, (dst, w, ws) in enumerate(((stage_g, w_gate, ws_gate), (stage_u, w_up, ws_up))):
                    for n in range(NH):
                        if routed:
                            sp.dma_start(dst[:, u % 2, n, :].rearrange("p (e i) -> p e i", i=I),
                                         w[8 * u:8 * u + 8, n * P:(n + 1) * P, :].rearrange("e p i -> p e i"))\
                                .then_inc(w_in[u][kind], 16)
                        else:
                            sp.dma_start(dst[:, u % 2, n, 0:SI], ws[n * P:(n + 1) * P, :]).then_inc(w_in[u][kind], 16)
                wd = w_down.rearrange("e i h -> (e i) h")[u * UW:(u + 1) * UW, :] if routed else ws_down
                tiles = wd.shape[0] // P
                sp.dma_start(stage_d[:, u % 2, 0:tiles, :], wd.rearrange("(t p) h -> p t h", p=P))\
                    .then_inc(w_in[u][2], 16)
                if u == 0:
                    for s in range(SPC):
                        sp.dma_start(x_tok[s * B:(s + 1) * B, 1:NC, :], steps[s, :, 1:NC, :]).then_inc(x_in, 16)
                    sp.dma_start(router[:, :, :], router_w.rearrange("(n p) e -> p n e", p=P)).then_inc(router_in, 16)

            outs = out.rearrange("b (c s) h -> c s b h", s=SPC)
            for c in range(NC):
                sp.wait_ge(res_ok, c + 1)
                for s in range(SPC):
                    sp.dma_start(outs[c, s], x_tok[s * B:(s + 1) * B, c, :]).then_inc(out_sent, 16)
            sp.wait_ge(out_sent, 16 * NC * SPC)

        @block.gpsimd
        def _(pool):
            nc.gpsimd.memset(identf[:, :], 0.0).then_inc(zeroed, 1)
            nc.gpsimd.memset(ident16[:, :], 0.0).then_inc(zeroed, 1)
            pool.wait_ge(zeroed, 2)
            for m in (identf, ident16):
                nc.gpsimd.affine_select(out=m[:, :], in_=m[:, :], compare_op=ALU.not_equal, fill=1.0, base=0,
                                        pattern=[[-1, P]], channel_multiplier=1).then_inc(ident_ok, 1)

            def sums(c, s, k):
                n, done = c * STG + 4 * s + k, c * SPC + s
                add, sub = ALU.add, ALU.subtract
                tt = nc.gpsimd.tensor_tensor
                q, d = arg(s, 0), drive_now[:, :, s, :]

                def tanh_low():
                    pool.wait_ge(th_ok, n + 1)
                    tt(th_lo[:, :, :], th[:, :, :], th_hi[:, :, :], sub).then_inc(th_lo_ok, 1)

                pool.wait_ge(y_ok, n + 1)
                if k == 0:
                    if s == 0:
                        pool.wait_ge(drive_now_ok, c + 1)
                    tt(qd_half[:, :, :], q, d, add).then_inc(qd_ok, 1)
                    tanh_low()
                    pool.wait_ge(qd_ok, 2 * done + 1)
                    pool.wait_ge(p_ok, n + 1)
                    tt(qdp[:, 0, :, :], qd_half[:, :, :], pk[:, 0, :, :], sub).then_inc(qdp_pool, 1)
                    tt(qd_full[:, :, :], qd_half[:, :, :], d, add).then_inc(qd_ok, 1)
                    return
                if k == 1:
                    pool.wait_ge(p_ok, n + 1)
                    tt(qdp[:, 1, :, :], qd_half[:, :, :], pk[:, 1, :, :], sub).then_inc(qdp_pool, 1)
                    tanh_low()
                    tt(dq[:, 0, :, :], arg(s, k), q, sub).then_inc(dq_ok, 1)
                    pool.wait_ge(dq_ok, 3 * done + 1)
                    tt(dsum[:, 0, :, :], dq[:, 0, :, :], d, add).then_inc(dsum_ok, 1)
                    return
                tt(dq[:, k - 1, :, :], arg(s, k), q, sub).then_inc(dq_ok, 1)
                tanh_low()
                pool.wait_ge(dq_ok, 3 * done + k)
                for i in (1, 2) if k == 2 else (3,):
                    pool.wait_ge(dsum_ok, 4 * done + i)
                    tt(dsum[:, i, :, :], dsum[:, i - 1, :, :], dq[:, k - 1, :, :], add).then_inc(dsum_ok, 1)

            def q_low(c, s):
                n = c * SPC + s + 1
                pool.wait_ge(y_ok, 4 * n + 1)
                pool.wait_ge(qhi_ok, n)
                if s == 0 and not first(c):
                    pool.wait_ge(tok_ok, 2 * c)
                nc.gpsimd.tensor_tensor(q_lo[:, :, s, :], q_new[:, :, s, :], q_hi[:, :, s, :], ALU.subtract)\
                    .then_inc(qlo_ok, 1)

            def chunk(c):
                for s in range(SPC):
                    for k in range(4):
                        sums(c, s, k)
                        if k == 0 and s > 0:
                            q_low(c, s - 1)
                q_low(c, SPC - 1)

            nc.gpsimd.memset(logit[:, :], LOW).then_inc(consts_ok, 1)

            chunk(0)
            with pool.Fori(1, NC) as c:
                chunk(c)

        @block.scalar
        def _(act):
            act.wait_ge(coup_mm, 1)
            nc.scalar.activation(coup_hi[:, :, :], ps_gate[0][:, :].rearrange("p (n m) -> p n m", n=NH), ACT.Copy,
                                 scale=WSCALE).then_inc(coup_hi_ok, 1)
            act.wait_ge(bias_mm, 1)
            nc.scalar.activation(bias_dt[:, :], ps_misc[:, 0:NH], ACT.Copy, scale=DT / 2, bias=-PSHIFT * DT / 2)\
                .then_inc(bias_ok, 1)
            act.wait_ge(bias_ok, 1)

            def drive_of(c):
                act.wait_ge(xT_mm, c + 1)
                for n in range(NH):
                    nc.scalar.activation(drive[:, c, n, :, :], ps_xT(c, n).rearrange("p (s b) -> p s b", b=B),
                                         ACT.Identity, scale=DT / 2, bias=bias_dt[:, n:n + 1]).then_inc(drive_ok, 1)

            def tanh(c, s, k):
                act.wait_ge(y_ok, c * STG + 4 * s + k + 1)
                nc.scalar.activation(th_hi[:, :, :], arg(s, k), ACT.Tanh).then_inc(th_hi_ok, 1)
                nc.scalar.activation(th[:, :, :], arg(s, k), ACT.Tanh).then_inc(th_ok, 1)
                nc.scalar.activation(sq[:, :, :], arg(s, k), ACT.Square).then_inc(sq_ok, 1)

            def q_high(c, s):
                act.wait_ge(y_ok, 4 * (c * SPC + s + 1) + 1)
                if s == 0 and not first(c):
                    act.wait_ge(tok_ok, 2 * c)
                nc.scalar.activation(q_hi[:, :, s, :], q_new[:, :, s, :], ACT.Copy).then_inc(qhi_ok, 1)

            def split_high(piece):
                u, kind, n = piece // (3 * NH), piece // NH % 3, piece % NH
                if n == 0:
                    act.wait_ge(w_in[u][kind], 16 if kind == 2 else 16 * NH)
                src, hi, _ = weight_piece(u, kind, n)
                nc.scalar.activation(hi, src, ACT.Copy, scale=WSCALE).then_inc(w_hi_ok, 1)

            def silu_of(f, g):
                act.wait_ge(gate_mm, NG * f + g + 1)
                if g >= 2:
                    act.wait_ge(hid_ok, NG * f + g - 1)
                elif not first(f):
                    act.wait_ge(hid_ok, NG * f)
                nc.scalar.activation(silu[:, g % 2, :], ps_gate[g % 2][:, :], ACT.Silu, scale=1 / WSCALE)\
                    .then_inc(silu_ok, 1)

            def hidden_high(f, g):
                act.wait_ge(hid_ok, NG * f + g + 1)
                nc.scalar.activation(hid_hi[:, g, :], hid[:, g, :], ACT.Copy).then_inc(hhi_ok, 1)

            def hidden_turned(f, g, j):
                act.wait_ge(hidT_mm, NG * f + g + 1)
                half = slice(j * GT, (j + 1) * GT)
                nc.scalar.activation(hidT[:, g, half, :], ps_hidT[:, half, :], ACT.Copy).then_inc(hidT_ok, 1)

            def route_tanh(f):
                act.wait_ge(half_ok, f + 1)
                nc.scalar.activation(tz[:, :], logit[:, 0:E], ACT.Tanh, scale=0.5, bias=half_max[:, 0:1])\
                    .then_inc(tz_ok, 1)

            def ffn_work(f, items):
                for kind, g, j in items:
                    if kind == "silu":
                        silu_of(f, g)
                    elif kind == "high":
                        hidden_high(f, g)
                    else:
                        hidden_turned(f, g, j)

            def chunk(c, scan, ffn, pieces, before=True):
                for i in range(STG):
                    s, k = i // 4, i % 4
                    if scan:
                        tanh(c, s, k)
                        if k == 0 and s > 0:
                            q_high(c, s - 1)
                    if ffn and i == 2:
                        route_tanh(c - 1)
                    for piece in pieces[i]:
                        split_high(piece)
                    if scan and not ffn and i > STG - NC:
                        drive_of(i - (STG - NC))
                    if ffn and before:
                        ffn_work(c - 2, SCALAR[i + STG])
                    if ffn:
                        ffn_work(c - 1, SCALAR[i])
                if scan:
                    q_high(c, SPC - 1)

            drive_of(0)
            chunk(0, True, False, PIECES_0)
            chunk(1, True, True, PIECES_1, before=False)
            with act.Fori(2, NC) as c:
                chunk(c, True, True, NO_PIECES)
            chunk(NC, False, True, NO_PIECES)
            for i in range(STG, 2 * STG):
                ffn_work(NC - 1, SCALAR[i])

        @block.vector
        def _(dve):
            stt, tt, ts = nc.vector.scalar_tensor_tensor, nc.vector.tensor_tensor, nc.vector.tensor_scalar

            dve.wait_ge(coup_hi_ok, 1)
            stt(out=coup_lo[:, :, :], in0=ps_gate[0][:, :].rearrange("p (n m) -> p n m", n=NH), scalar=WSCALE,
                in1=coup_hi[:, :, :], op0=ALU.mult, op1=ALU.subtract).then_inc(coup_lo_ok, 1)
            dve.wait_ge(cond_mm, 1)
            c0 = ps_coupled
            nc.vector.tensor_copy(q_new[:, :, SPC - 1, :], c0).then_inc(y_ok, 1)
            ts(pk[:, 0, :, :], c0, -PSHIFT, DT / 2, ALU.add, ALU.mult).then_inc(p_ok, 1)

            def before_coupling(c, s, k):
                n, done = c * STG + 4 * s + k, c * SPC + s
                yk, q = arg(s, k), arg(s, 0)
                dve.wait_ge(y_ok, n + 1)
                dve.wait_ge(p_ok, n + 1)
                stt(out=slope[:, :, :], in0=pk[:, k, :, :], scalar=-BETA * 2 / DT, in1=yk, op0=ALU.mult, op1=ALU.add)\
                    .then_inc(slope_ok, 1)
                if k >= 2:
                    if k == 2:
                        dve.wait_ge(qd_ok, 2 * done + 2)
                    stt(out=qdp[:, k, :, :], in0=pk[:, k, :, :], scalar=-CQ[k] * 2 / DT,
                        in1=qd_full[:, :, :] if k == 2 else q, op0=ALU.mult, op1=ALU.add).then_inc(qdp_ok, 1)
                dve.wait_ge(sq_ok, n + 1)
                stt(out=cubic[:, :, :], in0=sq[:, :, :], scalar=-3.0, in1=yk, op0=ALU.add, op1=ALU.mult)\
                    .then_inc(cubic_ok, 1)
                dve.wait_ge(slope_ok, n + 1)
                if k < 3:
                    stt(out=pk[:, k + 1, :, :], in0=slope[:, :, :], scalar=CP[k] * DT / 2, in1=pk[:, 0, :, :],
                        op0=ALU.mult, op1=ALU.add).then_inc(p_ok, 1)
                if k > 0:
                    dve.wait_ge(pacc_ok, 4 * done + k)
                stt(out=pacc[:, k, :, :], in0=slope[:, :, :], scalar=CPSUM[k] * DT / 2,
                    in1=pacc[:, k - 1, :, :] if k > 0 else pk[:, 0, :, :],
                    op0=ALU.mult, op1=ALU.add).then_inc(pacc_ok, 1)
                dve.wait_ge(cubic_ok, n + 1)
                if k < 2:
                    dve.wait_ge(qdp_pool, 2 * done + k + 1)
                else:
                    dve.wait_ge(qdp_ok, 2 * done + k - 1)
                stt(out=base[:, :, :], in0=cubic[:, :, :], scalar=-CQ[k] / 3, in1=qdp[:, k, :, :],
                    op0=ALU.mult, op1=ALU.add).then_inc(base_ok, 1)
                dve.wait_ge(base_ok, n + 1)
                if k == 3:
                    dve.wait_ge(dsum_ok, 4 * (done + 1))
                    stt(out=base3[:, :, :], in0=dsum[:, 3, :, :], scalar=1 / 3, in1=base[:, :, :],
                        op0=ALU.mult, op1=ALU.add).then_inc(base3_ok, 1)
                    dve.wait_ge(pacc_ok, 4 * (done + 1))
                    ts(pk[:, 0, :, :], pacc[:, 3, :, :], (CLAMP - PSHIFT) * DT / 2, (-CLAMP - PSHIFT) * DT / 2, ALU.min, ALU.max)\
                        .then_inc(p_ok, 1)
                    dve.wait_ge(base3_ok, done + 1)

            def after_coupling(c, s, k):
                n, done = c * STG + 4 * s + k, c * SPC + s
                dve.wait_ge(coupled, n + 1)
                if k < 3:
                    stt(out=y[:, k, :, :], in0=ps_coupled, scalar=CQ[k] / WSCALE, in1=base[:, :, :],
                        op0=ALU.mult, op1=ALU.add).then_inc(y_ok, 1)
                    return
                stt(out=q_raw[:, :, :], in0=ps_coupled, scalar=CQ[3] / WSCALE, in1=base3[:, :, :],
                    op0=ALU.mult, op1=ALU.add).then_inc(raw_ok, 1)
                dve.wait_ge(raw_ok, done + 1)
                if s == 0 and not first(c):
                    dve.wait_ge(logit_mm, c)
                ts(q_new[:, :, s, :], q_raw[:, :, :], CLAMP, -CLAMP, ALU.min, ALU.max).then_inc(y_ok, 1)

            def copy_chunk(c):
                if not first(c):
                    dve.wait_ge(up_mm, NG * c)
                dve.wait_ge(qhi_ok, SPC * (c + 1))
                nc.vector.tensor_copy(tok_hi[:, :, :], q_hi[:, :, :, :].rearrange("p n s b -> p n (s b)"))\
                    .then_inc(tok_ok, 1)
                dve.wait_ge(qlo_ok, SPC * (c + 1))
                nc.vector.tensor_copy(tok_lo[:, :, :], q_lo[:, :, :, :].rearrange("p n s b -> p n (s b)"))\
                    .then_inc(tok_ok, 1)

            def split_low(piece):
                u, kind, n = piece // (3 * NH), piece // NH % 3, piece % NH
                dve.wait_ge(w_hi_ok, piece + 1)
                src, hi, lo = weight_piece(u, kind, n)
                stt(out=lo, in0=src, scalar=WSCALE, in1=hi, op0=ALU.mult, op1=ALU.subtract).then_inc(w_lo_ok, 1)

            LINKS = 10

            def route_pick(f):
                r = LINKS * f
                dve.wait_ge(logit_mm, f + 1)
                if first(f):
                    dve.wait_ge(consts_ok, 1)
                nc.vector.tensor_copy(logit[:, 0:E], ps_logit).then_inc(route_step, 1)
                nc.vector.max(out=top8[:, :], in_=ps_logit).then_inc(route_step, 1)
                dve.wait_ge(route_step, r + 2)
                nc.vector.memset(top8[:, TOPK:8], LOW).then_inc(route_step, 1)
                dve.wait_ge(route_step, r + 3)
                ts(half_max[:, :], top8[:, 0:1], -0.5, None, ALU.mult).then_inc(half_ok, 1)
                nc.vector.match_replace(out=marked[:, :], in_to_replace=top8[:, :], in_values=logit[:, :],
                                        imm_value=HIGH).then_inc(route_step, 1)

            def route_weights(f):
                r = LINKS * f
                if not first(f):
                    dve.wait_ge(hid_ok, NG * f)
                dve.wait_ge(tz_ok, f + 1)
                ts(ez_den[:, :], tz[:, :], -1.0, 1.0, ALU.mult, ALU.add).then_inc(route_step, 1)
                dve.wait_ge(route_step, r + 5)
                nc.vector.reciprocal(ez_rec[:, :], ez_den[:, :]).then_inc(route_step, 1)
                dve.wait_ge(route_step, r + 6)
                stt(out=ez[:, :], in0=tz[:, :], scalar=1.0, in1=ez_rec[:, :], op0=ALU.add, op1=ALU.mult)\
                    .then_inc(route_step, 1)
                dve.wait_ge(route_step, r + 7)
                stt(out=ez_top[:, :], in0=marked[:, 0:E], scalar=HIGH, in1=ez[:, :], op0=ALU.is_ge, op1=ALU.mult,
                    accum_out=ez_sum[:, :]).then_inc(route_step, 1)
                dve.wait_ge(route_step, r + 8)
                nc.vector.reciprocal(ez_inv[:, :], ez_sum[:, :]).then_inc(route_step, 1)
                dve.wait_ge(route_step, r + 9)
                ts(comb[:, :], ez_top[:, :], ez_inv[:, 0:1], CSCALE, ALU.mult, ALU.mult).then_inc(route_step, 1)

            def hidden(f, g, j):
                if j == 0:
                    dve.wait_ge(silu_ok, NG * f + g + 1)
                    dve.wait_ge(up_mm, NG * f + g + 1)
                    if g == 0:
                        dve.wait_ge(route_step, LINKS * (f + 1))
                e, a, b = segments(g)[j]
                last = stt(out=hid[:, g, a:b], in0=ps_up[g % 2][:, a:b],
                           scalar=CSCALE if e is None else comb[:, e:e + 1], in1=silu[:, g % 2, a:b],
                           op0=ALU.mult, op1=ALU.mult)
                if j == len(segments(g)) - 1:
                    last.then_inc(hid_ok, 1)

            def hidden_low(f, g, j):
                if j == 0:
                    dve.wait_ge(hhi_ok, NG * f + g + 1)
                half = slice(j * GC // 2, (j + 1) * GC // 2)
                tt(hid_lo[:, g, half], hid[:, g, half], hid_hi[:, g, half], ALU.subtract).then_inc(hlo_ok, 1)

            def finish(f, j):
                if j == 0:
                    dve.wait_ge(down_mm, NG * (f + 1))
                    tt(part[:, :], ps_out[:, H:2 * H], x_tok[:, f, :], ALU.add).then_inc(part_ok, 1)
                else:
                    dve.wait_ge(part_ok, f + 1)
                    tt(x_tok[:, f, :], ps_out[:, 0:H], part[:, :], ALU.add).then_inc(res_ok, 1)

            def ffn_work(f, items):
                for kind, g, j in items:
                    if kind == "product":
                        hidden(f, g, j)
                    elif kind == "low":
                        hidden_low(f, g, j)
                    else:
                        finish(f, j)

            def chunk(c, scan, ffn, pieces, before=True):
                if scan:
                    if isinstance(c, int):
                        dve.wait_ge(drive_ok, NH * (1 if c == 0 else NC))
                    if not first(c):
                        dve.wait_ge(dsum_ok, 4 * SPC * c)
                    nc.vector.tensor_copy(drive_now[:, :, :, :], drive[:, c, :, :, :]).then_inc(drive_now_ok, 1)
                for i in range(STG):
                    s, k = i // 4, i % 4
                    if scan:
                        before_coupling(c, s, k)
                    for piece in pieces[i]:
                        split_low(piece)
                    if ffn and before:
                        ffn_work(c - 2, VECTOR[i + STG])
                    if ffn:
                        ffn_work(c - 1, VECTOR[i])
                    if scan:
                        after_coupling(c, s, k)
                    if ffn and i == 1:
                        route_pick(c - 1)
                    if ffn and i == 2:
                        route_weights(c - 1)
                if scan:
                    copy_chunk(c)

            chunk(0, True, False, PIECES_0)
            chunk(1, True, True, PIECES_1, before=False)
            with dve.Fori(2, NC) as c:
                chunk(c, True, True, NO_PIECES)
            chunk(NC, False, True, NO_PIECES)
            for i in range(STG, 2 * STG):
                ffn_work(NC - 1, VECTOR[i])

        @block.tensor
        def _(pe):
            mm = nc.tensor.matmul

            def x_transposed(c):
                if c == 0:
                    pe.wait_ge(x0_in, 16 * SPC)
                elif c == 1:
                    pe.wait_ge(x_in, 16 * SPC)
                if c >= 4:
                    pe.wait_ge(drive_ok, NH * (c - 3))
                for n in range(NH):
                    last = nc.tensor.transpose(ps_xT(c, n), x_tok[:, c, n * P:(n + 1) * P], identf[:, :])
                last.then_inc(xT_mm, 1)

            def couple(c, s, k):
                n = c * STG + 4 * s + k
                pe.wait_ge(th_hi_ok, n + 1)
                for m in range(NH):
                    to = slice(m * P, (m + 1) * P)
                    acc = ps_scan[:, m * B:(m + 1) * B]
                    mm(acc, coup_hi[:, 0, to], th_hi[:, 0, :], start=True, stop=False)
                    mm(acc, coup_hi[:, 1, to], th_hi[:, 1, :], start=False, stop=False)
                    mm(acc, coup_lo[:, 0, to], th_hi[:, 0, :], start=False, stop=False)
                    mm(acc, coup_lo[:, 1, to], th_hi[:, 1, :], start=False, stop=False)
                    pe.wait_ge(th_lo_ok, n + 1)
                    mm(acc, coup_hi[:, 0, to], th_lo[:, 0, :], start=False, stop=False)
                    last = mm(acc, coup_hi[:, 1, to], th_lo[:, 1, :], start=False, stop=True)
                last.then_inc(coupled, 1)

            def project(ps, hi, lo, g, i):
                n, term = i // 3, i % 3
                tok, w = ((tok_hi, hi), (tok_hi, lo), (tok_lo, hi))[term]
                return mm(ps[:, :], tok[:, n, :], w[:, n, g * GC:(g + 1) * GC], start=(i == 0), stop=(i == 3 * NH - 1))

            def unit(f, kind, g, i, weights_new):
                n = NG * f + g
                if kind == "gate":
                    if i == 0:
                        if g == 0:
                            pe.wait_ge(tok_ok, 2 * (f + 1))
                        if weights_new:
                            pe.wait_ge(w_lo_ok, pieces_for(g))
                        if g >= 2:
                            pe.wait_ge(silu_ok, n - 1)
                        elif g == 0 and not first(f):
                            pe.wait_ge(silu_ok, n)
                    last = project(ps_gate[g % 2], wg_hi, wg_lo, g, i)
                    if i == 3 * NH - 1:
                        last.then_inc(gate_mm, 1)
                elif kind == "up":
                    if i == 0:
                        if g >= 2:
                            pe.wait_ge(hid_ok, n - 1)
                        elif g == 0 and not first(f):
                            pe.wait_ge(hid_ok, n)
                    last = project(ps_up[g % 2], wu_hi, wu_lo, g, i)
                    if i == 3 * NH - 1:
                        last.then_inc(up_mm, 1)
                elif kind == "turn":
                    pe.wait_ge(hlo_ok, 2 * (n + 1))
                    if g > 0 or not first(f):
                        pe.wait_ge(hidT_ok, 2 * n)
                    for t in range(2 * GT):
                        src = (hid_hi, hid_lo)[t // GT][:, g, t % GT * P:(t % GT + 1) * P]
                        last = nc.tensor.transpose(ps_hidT[:, t, :], src, ident16[:, :])
                    last.then_inc(hidT_mm, 1)
                else:
                    if i == 0:
                        pe.wait_ge(hidT_ok, 2 * (n + 1))
                        if g == 0 and not first(f):
                            pe.wait_ge(res_ok, f)
                    tile, final = g * GT + i, g == NG - 1 and i == GT - 1
                    mm(ps_out[:, :], hidT[:, g, i, :], wd[:, tile, :, :].rearrange("p a h -> p (a h)"),
                       start=(g == 0 and i == 0), stop=False, skip_group_check=True)
                    last = mm(ps_out[:, H:2 * H], hidT[:, g, GT + i, :], wd[:, tile, 0, :],
                              start=False, stop=final, skip_group_check=True)
                    if i == GT - 1:
                        last.then_inc(down_mm, 1)

            def logits(f):
                for n in range(NH):
                    last = mm(ps_logit, q_new[:, n, :, :].rearrange("p s b -> p (s b)"), router[:, n, :],
                              start=(n == 0), stop=(n == NH - 1))
                last.then_inc(logit_mm, 1)

            def chunk(c, scan, ffn, weights_new=False, before=True):
                if ffn:
                    if weights_new:
                        pe.wait_ge(router_in, 16)
                        pe.wait_ge(drive_ok, NH * NC)
                    pe.wait_ge(y_ok, c * STG + 1)
                    logits(c - 1)
                for i in range(STG):
                    s, k = i // 4, i % 4
                    if scan:
                        couple(c, s, k)
                    if scan and not ffn and i > STG - NC:
                        x_transposed(i - (STG - NC))
                    if ffn and before:
                        for kind, g, j in MATRIX[i + STG]:
                            unit(c - 2, kind, g, j, False)
                    if ffn:
                        for kind, g, j in MATRIX[i]:
                            unit(c - 1, kind, g, j, weights_new)

            pe.wait_ge(ident_ok, 2)
            pe.wait_ge(coup_in, 16)
            for n in range(NH):
                for m in range(NH):
                    last = nc.tensor.transpose(ps_gate[0][:, n * H + m * P:n * H + (m + 1) * P],
                                               coup_row[:, m, n * P:(n + 1) * P], identf[:, :])
            last.then_inc(coup_mm, 1)
            pe.wait_ge(cond_in, 16)
            for n in range(NH):
                last = nc.tensor.transpose(ps_scan[:, n * B:(n + 1) * B], cond_row[:, n * P:(n + 1) * P],
                                           identf[0:B, 0:B])
            last.then_inc(cond_mm, 1)
            pe.wait_ge(bias_in, 16)
            nc.tensor.transpose(ps_misc[:, 0:NH], bias_row[:, :], identf[0:NH, 0:NH]).then_inc(bias_mm, 1)
            x_transposed(0)
            pe.wait_ge(coup_lo_ok, 1)
            pe.wait_ge(p_ok, 1)

            chunk(0, True, False)
            chunk(1, True, True, weights_new=True, before=False)
            with pe.Fori(2, NC) as c:
                chunk(c, True, True)
            chunk(NC, False, True)
            for i in range(STG, 2 * STG):
                for kind, g, j in MATRIX[i]:
                    unit(NC - 1, kind, g, j, False)


_INS = ["x", "cond_2048", "L0_cond_coupling", "L0_cond_bias", "L0_ffn_router_w", "L0_ffn_w_gate", "L0_ffn_w_up",
        "L0_ffn_w_down", "L0_ffn_ws_gate", "L0_ffn_ws_up", "L0_ffn_ws_down"]
_OUTS = [((B, T, H), "float32")]


def kernel(**inputs):
    import numpy as _np
    import concourse.bacc as _bacc
    from concourse import mybir as _mybir
    from concourse.bass_utils import run_bass_kernel_spmd as _run

    nc = _bacc.Bacc("TRN2", target_bir_lowering=False, num_devices=1)
    arrays, args = {}, []
    for name in _INS:
        a = _np.ascontiguousarray(inputs[name])
        arrays[f"in_{name}_dram"] = a
        args.append(nc.dram_tensor(f"in_{name}_dram", a.shape, _mybir.dt.from_np(a.dtype), kind="ExternalInput").ap())
    for i, (shape, dtype) in enumerate(_OUTS):
        dt = _mybir.dt.from_np(_np.dtype(dtype))
        args.append(nc.dram_tensor(f"out_{i}_dram", shape, dt, kind="ExternalOutput").ap())
    build(nc, *args)
    r = _run(nc, [arrays], core_ids=[0])
    return r.results[0]["out_0_dram"]
```

```python
import concourse.bass as bass
from concourse import mybir
from contextlib import ExitStack

F32 = mybir.dt.float32
F16 = mybir.dt.float16
ALU = mybir.AluOpType
ACT = mybir.ActivationFunctionType

P = 128
B, T, H = 32, 32, 256
E, I, SI, TOPK = 32, 96, 512, 4
NH = H // P
SPC = P // B
NC = T // SPC
SW = NH * B
GT = 4
GC = GT * P
NG = (E * I + SI) // GC
NGR = E * I // GC
UW = 8 * I
NU = E // 8 + 1
GATE, UP, DOWN = range(3)
ORDER = [(0, GATE), (0, UP), (1, GATE), (1, UP), (2, GATE), (2, UP), (3, GATE), (3, UP), (0, DOWN),
         (4, GATE), (4, UP), (1, DOWN), (2, DOWN), (3, DOWN), (4, DOWN)]
HID = NG * GC
STG = 4 * SPC

DT, EPS, ALPHA, BETA, CLAMP = 0.01, 0.08, 0.7, 0.8, 20.0
CQ = [DT / 2, DT / 2, DT, DT / 6]
CP = [v * EPS for v in CQ]
PSHIFT = ALPHA / BETA
PY = [v * DT / 2 for v in CP]
PP = [-v * BETA for v in CP]

WSCALE = 16.0
CSCALE = 1.0 / WSCALE / 16.0
LOW = -1.0e30
HIGH = 1.0e30


def build(nc, x, cond, coupling, bias, router_w, w_gate, w_up, w_down, ws_gate, ws_up, ws_down, out):
    ctx = ExitStack()
    with ctx:
        def sb(name, shape, dt=F32):
            return ctx.enter_context(nc.sbuf_tensor(name, shape, dt))

        def pb(name, shape, dt=F32):
            return ctx.enter_context(nc.psum_tensor(name, shape, dt))

        def sem(name):
            return ctx.enter_context(nc.semaphore(name))

        x_tok = sb("x_tok", [P, NC, H])
        drive = sb("drive", [P, NC, NH, SPC, B])
        drive_now = sb("drive_now", [P, NH, SPC, B])
        bias_row = sb("bias_row", [NH, P])
        bias_dt = sb("bias_dt", [P, NH])
        coup_row = sb("coup_row", [P, NH, H])
        coup_hi = sb("coup_hi", [P, NH, H], F16)
        coup_lo = sb("coup_lo", [P, NH, H], F16)
        router = sb("router", [P, NH, E])
        identf = sb("identf", [P, P])
        ident16 = sb("ident16", [P, P], F16)

        q_new = sb("q_new", [P, NH, SPC, B])
        q_raw = sb("q_raw", [P, NH, B])
        q_hi = sb("q_hi", [P, NH, SPC, B], F16)
        q_lo = sb("q_lo", [P, NH, SPC, B], F16)
        tok_hi = sb("tok_hi", [P, NH, SPC * B], F16)
        tok_lo = sb("tok_lo", [P, NH, SPC * B], F16)
        y = sb("y", [P, 3, NH, B])
        th = sb("th", [P, NH, B])
        th_hi = sb("th_hi", [P, NH, B], F16)
        th_lo = sb("th_lo", [P, NH, B], F16)
        sq = sb("sq", [P, NH, B])
        cubic = sb("cubic", [P, NH, B])
        base = sb("base", [P, NH, B])
        qdp = sb("qdp", [P, 4, NH, B])
        qd_half = sb("qd_half", [P, NH, B])
        qd_full = sb("qd_full", [P, NH, B])
        dq = sb("dq", [P, 3, NH, B])
        dsum = sb("dsum", [P, 4, NH, B])
        pk = sb("pk", [P, 4, NH, B])
        p0_weighed = sb("p0_weighed", [P, NH, B])
        p3_weighed = sb("p3_weighed", [P, NH, B])
        slope = sb("slope", [P, NH, B])
        psum = sb("psum", [P, 3, NH, B])
        p_three = sb("p_three", [P, NH, B])
        p_clip = sb("p_clip", [P, NH, B])

        stage_g = sb("stage_g", [P, 2, NH, UW])
        stage_u = sb("stage_u", [P, 2, NH, UW])
        stage_d = sb("stage_d", [P, 2, UW // P, H])
        wg_hi = sb("wg_hi", [P, NH, HID], F16)
        wg_lo = sb("wg_lo", [P, NH, HID], F16)
        wu_hi = sb("wu_hi", [P, NH, HID], F16)
        wu_lo = sb("wu_lo", [P, NH, HID], F16)
        wd = sb("wd", [P, HID // P, 2, H], F16)

        silu = sb("silu", [P, 4, GC])
        hid = sb("hid", [P, NG, GC])
        hid_hi = sb("hid_hi", [P, NG, GC], F16)
        hid_lo = sb("hid_lo", [P, NG, GC], F16)
        hidT = sb("hidT", [P, NG, 2 * GT, P], F16)

        logit = sb("logit", [P, E + TOPK])
        top8 = sb("top8", [P, 8])
        half_max = sb("half_max", [P, 1])
        tz = sb("tz", [P, E])
        ez_den = sb("ez_den", [P, E])
        ez_rec = sb("ez_rec", [P, E])
        ez = sb("ez", [P, E])
        marked = sb("marked", [P, E + TOPK])
        ez_top = sb("ez_top", [P, E])
        ez_sum = sb("ez_sum", [P, 1])
        ez_inv = sb("ez_inv", [P, 1])
        comb = sb("comb", [P, E])
        part = sb("part", [P, H])
        cond_row = part[0:B, :]
        primer = sb("primer", [P, 1])

        ps_gate = [pb(f"ps_gate{i}", [P, GC]) for i in range(2)]
        ps_up = [pb(f"ps_up{i}", [P, GC]) for i in range(3)]
        ps_hidT = pb("ps_hidT", [P, 2 * GT, P], F16)
        ps_out = pb("ps_out", [P, 2 * H])
        ps_scan = pb("ps_scan", [P, GC])
        ps_logit = ps_scan[:, SW:SW + E]
        ps_coupled = ps_scan[:, 0:SW].rearrange("p (n b) -> p n b", n=NH)

        cond_in, bias_in, coup_in, router_in = sem("cond_in"), sem("bias_in"), sem("coup_in"), sem("router_in")
        x0_in, x_in = sem("x0_in"), sem("x_in")
        w_in = [[sem(f"w{kind}_in{u}") for kind in "gud"] for u in range(NU)]
        zeroed, ident_ok, consts_ok, primed = sem("zeroed"), sem("ident_ok"), sem("consts_ok"), sem("primed")
        coup_mm, coup_hi_ok, coup_lo_ok, cond_mm, bias_mm = (
            sem("coup_mm"), sem("coup_hi_ok"), sem("coup_lo_ok"), sem("cond_mm"), sem("bias_mm"))
        bias_ok, xT_mm, drive_ok = sem("bias_ok"), sem("xT_mm"), sem("drive_ok")
        drive_now_ok = sem("drive_now_ok")
        w_hi_ok, w_lo_ok = sem("w_hi_ok"), sem("w_lo_ok")
        y_ok, pk_ok, coupled = sem("y_ok"), sem("pk_ok"), sem("coupled")
        th_hi_ok, th_ok, th_lo_ok = sem("th_hi_ok"), sem("th_ok"), sem("th_lo_ok")
        sq_ok, qd_ok, dq_ok, dsum_ok, dsum3_ok = (
            sem("sq_ok"), sem("qd_ok"), sem("dq_ok"), sem("dsum_ok"), sem("dsum3_ok"))
        qdp_pool, qdp_ok = sem("qdp_pool"), sem("qdp_ok")
        psum_ok, p_three_ok, p_clip_ok, p0_ok = sem("psum_ok"), sem("p_three_ok"), sem("p_clip_ok"), sem("p0_ok")
        p0_weighed_ok, p3_weighed_ok, slope_ok, cubic_ok, base_ok, raw_ok = (
            sem("p0_weighed_ok"), sem("p3_weighed_ok"), sem("slope_ok"), sem("cubic_ok"), sem("base_ok"), sem("raw_ok"))
        qhi_ok, qlo_ok, tok_ok = sem("qhi_ok"), sem("qlo_ok"), sem("tok_ok")
        gate_mm, up_mm, hidT_mm, down_mm = sem("gate_mm"), sem("up_mm"), sem("hidT_mm"), sem("down_mm")
        silu_ok, hid_ok, hhi_ok, hlo_ok, hidT_ok = (
            sem("silu_ok"), sem("hid_ok"), sem("hhi_ok"), sem("hlo_ok"), sem("hidT_ok"))
        logit_mm, route_step, tz_ok = sem("logit_mm"), sem("route_step"), sem("tz_ok")
        part_ok, res_ok, out_sent = sem("part_ok"), sem("res_ok"), sem("out_sent")

        def up_bank(g):
            return ps_up[g % 2 if g < NG - 1 else 2]

        def silu_slot(g):
            return silu[:, g % 3 if g < NG - 1 else 3, :]

        def first(c):
            return isinstance(c, int) and c == 0

        def arg(s, k):
            return q_new[:, :, (s - 1) % SPC, :] if k == 0 else y[:, k - 1, :, :]

        def split_count(u, kind):
            return NH * (ORDER.index((u, kind)) + 1)

        def split_for_group(g):
            return max(split_count(u, UP) for u in range(min(NU - 1, ((g + 1) * GC - 1) // UW) + 1))

        def split_for_tile(t):
            u = min(NU - 1, t * P // UW)
            tiles = (UW if u < NU - 1 else SI) // P
            return split_count(u, DOWN) - (1 if t - u * UW // P < tiles // NH else 0)

        def weight_piece(u, kind, n):
            width = UW if u < NU - 1 else SI
            if kind != DOWN:
                cols = slice(u * UW, u * UW + width)
                hi, lo = ((wg_hi, wg_lo), (wu_hi, wu_lo))[kind]
                return (stage_g, stage_u)[kind][:, u % 2, n, 0:width], hi[:, n, cols], lo[:, n, cols]
            half = width // P // NH
            tiles = slice(u * UW // P + n * half, u * UW // P + (n + 1) * half)
            return stage_d[:, u % 2, n * half:(n + 1) * half, :], wd[:, tiles, 0, :], wd[:, tiles, 1, :]

        HIGH_AT = [1, 2, 4, 5, 6, 8, 10, 11, 12, 12, 14, 15]
        HIGH_AT += [STG + i for i in (1, 1, 2, 3, 4, 4, 7, 8, 10, 10, 12, 14)]
        HIGH_AT += [2 * STG + i for i in (1, 2, 4, 5, 7, 8)]
        LOW_AT = [2, 3, 5, 6, 7, 9, 11, 12, 13, 14, 15]
        LOW_AT += [STG + i for i in (0, 2, 2, 3, 5, 5, 6, 9, 10, 12, 12, 14)]
        LOW_AT += [2 * STG + i for i in (0, 3, 3, 5, 7, 9, 10)]

        def pieces_at(at, c):
            return [[n for n, stage in enumerate(at) if stage == c * STG + i] for i in range(STG)]

        HIGH_PIECES = [pieces_at(HIGH_AT, c) for c in range(3)]
        LOW_PIECES = [pieces_at(LOW_AT, c) for c in range(3)]
        NO_PIECES = [[]] * STG

        def ps_xT(c, n):
            bank = (ps_gate[1], ps_up[0], ps_up[1], ps_out)[c % 4]
            return bank[:, n * P:(n + 1) * P]

        TURN_LAG, DOWN_LAG = 4, 6
        BLOCK = 3 * H * GT + 2 * 3 * NH * GC + 2 * GT * P

        STEP_ENDS = [0.24, 0.485, 0.73, 1.0]
        ENDS = [(s + end) / SPC for s in range(SPC) for end in STEP_ENDS]

        def slot_at(b, columns):
            at = (b * BLOCK + columns) / (NG * BLOCK)
            return int(at) * STG + sum(at % 1 >= end for end in ENDS)

        MATRIX = [[] for _ in range(2 * STG)]
        for b in range(NG + DOWN_LAG):
            cols = 0
            for i in range(GT):
                if b >= DOWN_LAG:
                    MATRIX[slot_at(b, cols)].append(("down", b - DOWN_LAG, i))
                cols += 3 * H
            for i in range(3 * NH):
                if b < NG:
                    MATRIX[slot_at(b, cols)].append(("gate", b, i))
                cols += GC
            for i in range(3 * NH):
                if b < NG:
                    MATRIX[slot_at(b, cols)].append(("up", b, i))
                cols += GC
            if TURN_LAG <= b < NG + TURN_LAG:
                MATRIX[slot_at(b, cols)].append(("turn", b - TURN_LAG, 0))
            cols += 2 * GT * P

        def after(kind, g):
            return max(i for i, units in enumerate(MATRIX) if any(u[:2] == (kind, g) for u in units)) + 1

        def segments(g):
            out, unit, end = [], g * GC, (g + 1) * GC
            while unit < end:
                e = unit // I
                stop = min(end, (e + 1) * I if e < E else unit + GC // 4)
                out.append((e if e < E else None, unit - g * GC, stop - g * GC))
                unit = stop
            return out

        ROUTE_PICK = 1
        ROUTE_AT = [1, 1, 1, 1, 1, 2, 2, 2, 3, 3, 3]
        LINKS = len(ROUTE_AT)

        VECTOR, SCALAR = ([[] for _ in range(2 * STG)] for _ in range(2))
        vector_load, scalar_load = [0, 0, 0, 200] * SPC, [0] * STG
        for link, i in enumerate(ROUTE_AT):
            VECTOR[i].append(("route", link, 0))
            vector_load[i] += 90
        VECTOR_ROOM, SCALAR_ROOM = 1040, 1220

        def place(table, load, room, item, columns, slot):
            while load[slot % STG] + columns > room:
                slot += 1
            load[slot % STG] += columns
            table[slot].append(item)
            return slot

        at = after("down", NG - 1)
        for j in range(2):
            at = place(VECTOR, vector_load, VECTOR_ROOM, ("finish", 0, j), H + 60, at)
        for g in range(NG):
            at = place(SCALAR, scalar_load, SCALAR_ROOM if g < NG - 1 else 2 * SCALAR_ROOM, ("silu", g, 0), GC,
                       min(after("gate", g), STG - 1))
            at = max(at, after("up", g) + 1)
            for j, (_, a, b) in enumerate(segments(g)):
                at = place(VECTOR, vector_load, VECTOR_ROOM, ("product", g, j), b - a + 100, at)
            at = place(SCALAR, scalar_load, SCALAR_ROOM, ("high", g, 0), GC, at + 1)
            for j in range(2):
                at = place(VECTOR, vector_load, VECTOR_ROOM, ("low", g, j), GC // 2 + 60, at + 1 - j)
            assert at <= after("turn", g) - 1
            at = after("turn", g)
            for j in range(2):
                at = place(SCALAR, scalar_load, SCALAR_ROOM, ("turned", g, j), GC, at)

        block = ctx.enter_context(nc.Block())

        @block.sync
        def _(sp):
            steps = x.rearrange("b (c s) h -> s b c h", s=SPC)
            sp.dma_start(coup_row[:, :, :], coupling.rearrange("(n p) k -> p n k", p=P)).then_inc(coup_in, 16)
            sp.dma_start(cond_row, cond).then_inc(cond_in, 16)
            sp.dma_start(bias_row[:, :], bias.rearrange("(n p) -> n p", p=P)).then_inc(bias_in, 16)
            for s in range(SPC):
                sp.dma_start(x_tok[s * B:(s + 1) * B, 0, :], steps[s, :, 0, :]).then_inc(x0_in, 16)
            for n, (u, kind) in enumerate(ORDER):
                if n == 3:
                    for s in range(SPC):
                        sp.dma_start(x_tok[s * B:(s + 1) * B, 1:NC, :], steps[s, :, 1:NC, :]).then_inc(x_in, 16)
                    sp.dma_start(router[:, :, :], router_w.rearrange("(n p) e -> p n e", p=P)).then_inc(router_in, 16)
                if u >= 2:
                    sp.wait_ge(w_hi_ok, split_count(u - 2, kind))
                    sp.wait_ge(w_lo_ok, split_count(u - 2, kind))
                routed = u < NU - 1
                if kind == DOWN:
                    wd_rows = w_down.rearrange("e i h -> (e i) h")[u * UW:(u + 1) * UW, :] if routed else ws_down
                    sp.dma_start(stage_d[:, u % 2, 0:wd_rows.shape[0] // P, :],
                                 wd_rows.rearrange("(t p) h -> p t h", p=P)).then_inc(w_in[u][kind], 16)
                    continue
                dst, w, ws = ((stage_g, w_gate, ws_gate), (stage_u, w_up, ws_up))[kind]
                for half in range(NH):
                    rows = slice(half * P, (half + 1) * P)
                    if routed:
                        sp.dma_start(dst[:, u % 2, half, :].rearrange("p (e i) -> p e i", i=I),
                                     w[8 * u:8 * u + 8, rows, :].rearrange("e p i -> p e i"))\
                            .then_inc(w_in[u][kind], 16)
                    else:
                        sp.dma_start(dst[:, u % 2, half, 0:SI], ws[rows, :]).then_inc(w_in[u][kind], 16)

            outs = out.rearrange("b (c s) h -> c s b h", s=SPC)
            for c in range(NC):
                sp.wait_ge(res_ok, c + 1)
                for s in range(SPC):
                    sp.dma_start(outs[c, s], x_tok[s * B:(s + 1) * B, c, :]).then_inc(out_sent, 16)
            sp.wait_ge(out_sent, 16 * NC * SPC)

        @block.gpsimd
        def _(pool):
            nc.gpsimd.memset(identf[:, :], 0.0).then_inc(zeroed, 1)
            nc.gpsimd.memset(ident16[:, :], 0.0).then_inc(zeroed, 1)
            pool.wait_ge(zeroed, 2)
            pool.wait_ge(primed, 1)
            for m in (identf, ident16):
                nc.gpsimd.affine_select(out=m[:, :], in_=m[:, :], compare_op=ALU.not_equal, fill=1.0, base=0,
                                        pattern=[[-1, P]], channel_multiplier=1).then_inc(ident_ok, 1)

            def sums(c, s, k):
                n, done = c * STG + 4 * s + k, c * SPC + s
                add, sub = ALU.add, ALU.subtract
                tt = nc.gpsimd.tensor_tensor
                q, d = arg(s, 0), drive_now[:, :, s, :]

                def tanh_low():
                    pool.wait_ge(th_ok, n + 1)
                    tt(th_lo[:, :, :], th[:, :, :], th_hi[:, :, :], sub).then_inc(th_lo_ok, 1)

                pool.wait_ge(y_ok, n + 1)
                if k == 0:
                    if s == 0 and first(c):
                        tanh_low()
                        pool.wait_ge(drive_ok, NH)
                        tt(qd_half[:, :, :], q, d, add).then_inc(qd_ok, 1)
                    else:
                        if s == 0:
                            pool.wait_ge(drive_now_ok, c)
                        tt(qd_half[:, :, :], q, d, add).then_inc(qd_ok, 1)
                        tanh_low()
                    pool.wait_ge(qd_ok, 2 * done + 1)
                    pool.wait_ge(p0_ok, done + 1)
                    tt(qdp[:, 0, :, :], qd_half[:, :, :], pk[:, 0, :, :], sub).then_inc(qdp_pool, 1)
                    tt(qd_full[:, :, :], qd_half[:, :, :], d, add).then_inc(qd_ok, 1)
                    return
                if k == 1:
                    pool.wait_ge(pk_ok, 3 * done + 1)
                    tt(qdp[:, 1, :, :], qd_half[:, :, :], pk[:, 1, :, :], sub).then_inc(qdp_pool, 1)
                    tanh_low()
                    tt(dq[:, 0, :, :], arg(s, k), q, sub).then_inc(dq_ok, 1)
                    pool.wait_ge(dq_ok, 3 * done + 1)
                    tt(dsum[:, 0, :, :], dq[:, 0, :, :], d, add).then_inc(dsum_ok, 1)
                    return
                if k == 2:
                    tt(dq[:, 1, :, :], arg(s, k), q, sub).then_inc(dq_ok, 1)
                    tanh_low()
                    pool.wait_ge(dq_ok, 3 * done + 2)
                    pool.wait_ge(dsum_ok, 4 * done + 1)
                    tt(dsum[:, 1, :, :], dsum[:, 0, :, :], dq[:, 1, :, :], add).then_inc(dsum_ok, 1)
                    pool.wait_ge(dsum_ok, 4 * done + 2)
                    tt(dsum[:, 0, :, :], dsum[:, 1, :, :], dq[:, 1, :, :], add).then_inc(dsum_ok, 1)
                    pool.wait_ge(pk_ok, 3 * (done + 1))
                    pool.wait_ge(dsum_ok, 4 * done + 3)
                    tt(dsum[:, 2, :, :], dsum[:, 0, :, :], pk[:, 3, :, :], sub).then_inc(dsum_ok, 1)
                    tt(psum[:, 0, :, :], pk[:, 1, :, :], pk[:, 2, :, :], add).then_inc(psum_ok, 1)
                    return
                tt(dq[:, 2, :, :], arg(s, k), q, sub).then_inc(dq_ok, 1)
                tanh_low()
                pool.wait_ge(psum_ok, 4 * done + 1)
                tt(psum[:, 1, :, :], psum[:, 0, :, :], pk[:, 2, :, :], add).then_inc(psum_ok, 1)
                pool.wait_ge(psum_ok, 4 * done + 2)
                tt(psum[:, 0, :, :], psum[:, 1, :, :], pk[:, 0, :, :], sub).then_inc(psum_ok, 1)
                pool.wait_ge(psum_ok, 4 * done + 3)
                pool.wait_ge(p3_weighed_ok, done + 1)
                tt(psum[:, 2, :, :], psum[:, 0, :, :], p3_weighed[:, :, :], add).then_inc(psum_ok, 1)

            def q_low(c, s):
                n = c * SPC + s + 1
                pool.wait_ge(y_ok, 4 * n + 1)
                pool.wait_ge(qhi_ok, n)
                if s == 0 and not first(c):
                    pool.wait_ge(tok_ok, 2 * c)
                nc.gpsimd.tensor_tensor(q_lo[:, :, s, :], q_new[:, :, s, :], q_hi[:, :, s, :], ALU.subtract)\
                    .then_inc(qlo_ok, 1)

            def chunk(c):
                for s in range(SPC):
                    for k in range(4):
                        sums(c, s, k)
                        if k == 0 and s > 0:
                            q_low(c, s - 1)
                        elif k == 0 and not first(c):
                            q_low(c - 1, SPC - 1)

            nc.gpsimd.memset(logit[:, :], LOW).then_inc(consts_ok, 1)
            nc.gpsimd.memset(drive[:, NC - 1, :, :, :], 0.0).then_inc(consts_ok, 1)

            chunk(0)
            with pool.Fori(1, NC) as c:
                chunk(c)
            q_low(NC - 1, SPC - 1)

        @block.scalar
        def _(act):
            act.wait_ge(zeroed, 2)
            nc.scalar.activation(primer[:, :], identf[:, 0:1], ACT.Silu).then_inc(primed, 1)
            act.wait_ge(coup_mm, 1)
            nc.scalar.activation(coup_hi[:, :, :], ps_gate[0][:, :].rearrange("p (n m) -> p n m", n=NH), ACT.Copy,
                                 scale=WSCALE).then_inc(coup_hi_ok, 1)
            act.wait_ge(bias_mm, 1)
            nc.scalar.activation(bias_dt[:, :], ps_up[2][:, 0:NH], ACT.Copy, scale=DT / 2, bias=-PSHIFT * DT / 2)\
                .then_inc(bias_ok, 1)
            act.wait_ge(bias_ok, 1)

            def drive_of(c):
                act.wait_ge(xT_mm, c + 1)
                for n in range(NH):
                    to = drive_now[:, n, :, :] if c == 0 else drive[:, c - 1, n, :, :]
                    nc.scalar.activation(to, ps_xT(c, n).rearrange("p (s b) -> p s b", b=B),
                                         ACT.Identity, scale=DT / 2, bias=bias_dt[:, n:n + 1]).then_inc(drive_ok, 1)

            def tanh(c, s, k):
                act.wait_ge(y_ok, c * STG + 4 * s + k + 1)
                nc.scalar.activation(th_hi[:, :, :], arg(s, k), ACT.Tanh).then_inc(th_hi_ok, 1)
                nc.scalar.activation(th[:, :, :], arg(s, k), ACT.Tanh).then_inc(th_ok, 1)
                nc.scalar.activation(sq[:, :, :], arg(s, k), ACT.Square).then_inc(sq_ok, 1)

            def new_p(c, s):
                act.wait_ge(p_clip_ok, c * SPC + s)
                nc.scalar.activation(p0_weighed[:, :, :], p_clip[:, :, :], ACT.Copy, scale=(1 + PP[0]) / 3).then_inc(p0_weighed_ok, 1)
                nc.scalar.activation(pk[:, 0, :, :], p_clip[:, :, :], ACT.Copy, scale=1 / 3).then_inc(p0_ok, 1)

            def weigh_p3(c, s):
                act.wait_ge(pk_ok, 3 * (c * SPC + s + 1))
                nc.scalar.activation(p3_weighed[:, :, :], pk[:, 3, :, :], ACT.Copy, scale=1 + 3 * PP[3])\
                    .then_inc(p3_weighed_ok, 1)

            def q_high(c, s):
                act.wait_ge(y_ok, 4 * (c * SPC + s + 1) + 1)
                if s == 0 and not first(c):
                    act.wait_ge(tok_ok, 2 * c)
                nc.scalar.activation(q_hi[:, :, s, :], q_new[:, :, s, :], ACT.Copy).then_inc(qhi_ok, 1)

            def copy_chunk(c, after_ffn):
                if after_ffn:
                    act.wait_ge(up_mm, NG * c)
                act.wait_ge(qhi_ok, SPC * (c + 1))
                nc.scalar.activation(tok_hi[:, :, :], q_hi[:, :, :, :].rearrange("p n s b -> p n (s b)"), ACT.Copy)\
                    .then_inc(tok_ok, 1)
                act.wait_ge(qlo_ok, SPC * (c + 1))
                nc.scalar.activation(tok_lo[:, :, :], q_lo[:, :, :, :].rearrange("p n s b -> p n (s b)"), ACT.Copy)\
                    .then_inc(tok_ok, 1)

            def split_high(piece):
                (u, kind), n = ORDER[piece // NH], piece % NH
                if n == 0:
                    act.wait_ge(w_in[u][kind], 16 if kind == DOWN else 16 * NH)
                src, hi, _ = weight_piece(u, kind, n)
                nc.scalar.activation(hi, src, ACT.Copy, scale=WSCALE).then_inc(w_hi_ok, 1)

            def silu_of(f, g):
                act.wait_ge(gate_mm, NG * f + g + 1)
                if 3 <= g < NG - 1:
                    act.wait_ge(hid_ok, NG * f + g - 2)
                elif g < 3 and not first(f):
                    act.wait_ge(hid_ok, NG * f + g - 3)
                nc.scalar.activation(silu_slot(g), ps_gate[g % 2][:, :], ACT.Silu, scale=1 / WSCALE)\
                    .then_inc(silu_ok, 1)

            def hidden_high(f, g):
                act.wait_ge(hid_ok, NG * f + g + 1)
                nc.scalar.activation(hid_hi[:, g, :], hid[:, g, :], ACT.Copy).then_inc(hhi_ok, 1)

            def hidden_turned(f, g, j):
                act.wait_ge(hidT_mm, NG * f + g + 1)
                half = slice(j * GT, (j + 1) * GT)
                nc.scalar.activation(hidT[:, g, half, :], ps_hidT[:, half, :], ACT.Copy).then_inc(hidT_ok, 1)

            def route_tanh(f):
                act.wait_ge(route_step, LINKS * f + 4)
                nc.scalar.activation(tz[:, :], logit[:, 0:E], ACT.Tanh, scale=0.5, bias=half_max[:, 0:1])\
                    .then_inc(tz_ok, 1)

            def ffn_work(f, items):
                for kind, g, j in items:
                    if kind == "silu":
                        silu_of(f, g)
                    elif kind == "high":
                        hidden_high(f, g)
                    else:
                        hidden_turned(f, g, j)

            def chunk(c, scan, ffn, pieces, before=True):
                for i in range(STG):
                    s, k = i // 4, i % 4
                    if scan:
                        tanh(c, s, k)
                        if first(c) and i == 0:
                            drive_of(0)
                        if k == 0 and not (first(c) and s == 0):
                            new_p(c, s)
                        elif k == 3:
                            weigh_p3(c, s)
                        if k == 0 and s > 0:
                            q_high(c, s - 1)
                    if ffn and i == 0:
                        q_high(c - 1, SPC - 1)
                        copy_chunk(c - 1, before)
                    if ffn and i == ROUTE_PICK + 1:
                        route_tanh(c - 1)
                    for piece in pieces[i]:
                        split_high(piece)
                    if scan and not ffn and i > STG - NC:
                        drive_of(i - (STG - NC))
                    if ffn and before:
                        ffn_work(c - 2, SCALAR[i + STG])
                    if ffn:
                        ffn_work(c - 1, SCALAR[i])

            chunk(0, True, False, HIGH_PIECES[0])
            chunk(1, True, True, HIGH_PIECES[1], before=False)
            chunk(2, True, True, HIGH_PIECES[2])
            with act.Fori(3, NC) as c:
                chunk(c, True, True, NO_PIECES)
            chunk(NC, False, True, NO_PIECES)
            for i in range(STG, 2 * STG):
                ffn_work(NC - 1, SCALAR[i])

        @block.vector
        def _(dve):
            stt, tt, ts = nc.vector.scalar_tensor_tensor, nc.vector.tensor_tensor, nc.vector.tensor_scalar

            dve.wait_ge(cond_mm, 1)
            c0 = ps_coupled
            nc.vector.tensor_copy(q_new[:, :, SPC - 1, :], c0).then_inc(y_ok, 1)
            ts(p0_weighed[:, :, :], c0, -PSHIFT, DT / 2 * (1 + PP[0]), ALU.add, ALU.mult).then_inc(p0_weighed_ok, 1)
            ts(pk[:, 0, :, :], c0, -PSHIFT, DT / 2, ALU.add, ALU.mult).then_inc(p0_ok, 1)
            dve.wait_ge(coup_hi_ok, 1)
            stt(out=coup_lo[:, :, :], in0=ps_gate[0][:, :].rearrange("p (n m) -> p n m", n=NH), scalar=WSCALE,
                in1=coup_hi[:, :, :], op0=ALU.mult, op1=ALU.subtract).then_inc(coup_lo_ok, 1)

            def before_coupling(c, s, k):
                n, done = c * STG + 4 * s + k, c * SPC + s
                yk, q = arg(s, k), arg(s, 0)
                dve.wait_ge(y_ok, n + 1)
                if k in (1, 2):
                    dve.wait_ge(pk_ok, 3 * done + k)
                    stt(out=slope[:, :, :], in0=pk[:, k, :, :], scalar=-BETA * 2 / DT, in1=yk,
                        op0=ALU.mult, op1=ALU.add).then_inc(slope_ok, 1)
                if k == 2:
                    dve.wait_ge(qd_ok, 2 * done + 2)
                    stt(out=qdp[:, 2, :, :], in0=pk[:, 2, :, :], scalar=-2.0, in1=qd_full[:, :, :],
                        op0=ALU.mult, op1=ALU.add).then_inc(qdp_ok, 1)
                dve.wait_ge(sq_ok, n + 1)
                stt(out=cubic[:, :, :], in0=sq[:, :, :], scalar=-3.0, in1=yk, op0=ALU.add, op1=ALU.mult)\
                    .then_inc(cubic_ok, 1)
                if k == 0:
                    dve.wait_ge(p0_weighed_ok, done + 1)
                    stt(out=pk[:, 1, :, :], in0=yk, scalar=PY[0], in1=p0_weighed[:, :, :],
                        op0=ALU.mult, op1=ALU.add).then_inc(pk_ok, 1)
                elif k < 3:
                    dve.wait_ge(slope_ok, 2 * done + k)
                    stt(out=pk[:, k + 1, :, :], in0=slope[:, :, :], scalar=PY[k], in1=pk[:, 0, :, :],
                        op0=ALU.mult, op1=ALU.add).then_inc(pk_ok, 1)
                if k < 3:
                    dve.wait_ge(cubic_ok, n + 1)
                else:
                    dve.wait_ge(dsum_ok, 4 * (done + 1))
                    dve.wait_ge(dq_ok, 3 * (done + 1))
                    tt(dsum[:, 3, :, :], dsum[:, 2, :, :], dq[:, 2, :, :], ALU.add).then_inc(dsum3_ok, 1)
                    dve.wait_ge(dsum3_ok, done + 1)
                    stt(out=qdp[:, 3, :, :], in0=dsum[:, 3, :, :], scalar=1 / 3, in1=q,
                        op0=ALU.mult, op1=ALU.add).then_inc(qdp_ok, 1)
                if k < 2:
                    dve.wait_ge(qdp_pool, 2 * done + k + 1)
                else:
                    dve.wait_ge(qdp_ok, 2 * done + k - 1)
                stt(out=base[:, :, :], in0=cubic[:, :, :], scalar=-CQ[k] / 3, in1=qdp[:, k, :, :],
                    op0=ALU.mult, op1=ALU.add).then_inc(base_ok, 1)

            def after_coupling(c, s, k):
                n, done = c * STG + 4 * s + k, c * SPC + s
                dve.wait_ge(base_ok, n + 1)
                dve.wait_ge(coupled, n + 1)
                if k < 3:
                    stt(out=y[:, k, :, :], in0=ps_coupled, scalar=CQ[k] / WSCALE, in1=base[:, :, :],
                        op0=ALU.mult, op1=ALU.add).then_inc(y_ok, 1)
                    return
                stt(out=q_raw[:, :, :], in0=ps_coupled, scalar=CQ[3] / WSCALE, in1=base[:, :, :],
                    op0=ALU.mult, op1=ALU.add).then_inc(raw_ok, 1)
                dve.wait_ge(raw_ok, done + 1)
                if s == 0 and not first(c):
                    dve.wait_ge(logit_mm, c)
                ts(q_new[:, :, s, :], q_raw[:, :, :], CLAMP, -CLAMP, ALU.min, ALU.max).then_inc(y_ok, 1)
                dve.wait_ge(psum_ok, 4 * (done + 1))
                stt(out=p_three[:, :, :], in0=y[:, 2, :, :], scalar=3 * PY[3], in1=psum[:, 2, :, :],
                    op0=ALU.mult, op1=ALU.add).then_inc(p_three_ok, 1)
                dve.wait_ge(p_three_ok, done + 1)
                ts(p_clip[:, :, :], p_three[:, :, :], 3 * (CLAMP - PSHIFT) * DT / 2, 3 * (-CLAMP - PSHIFT) * DT / 2,
                   ALU.min, ALU.max).then_inc(p_clip_ok, 1)

            def next_drive(c):
                if first(c):
                    dve.wait_ge(drive_ok, NH * NC)
                    dve.wait_ge(consts_ok, 2)
                dve.wait_ge(dsum_ok, 4 * (SPC * (c + 1) - 1) + 1)
                nc.vector.tensor_copy(drive_now[:, :, :, :], drive[:, c, :, :, :]).then_inc(drive_now_ok, 1)

            def split_low(piece):
                (u, kind), n = ORDER[piece // NH], piece % NH
                dve.wait_ge(w_hi_ok, piece + 1)
                src, hi, lo = weight_piece(u, kind, n)
                stt(out=lo, in0=src, scalar=WSCALE, in1=hi, op0=ALU.mult, op1=ALU.subtract).then_inc(w_lo_ok, 1)

            def route(f, link):
                def after_links(n):
                    dve.wait_ge(route_step, LINKS * f + n)

                if link == 0:
                    dve.wait_ge(logit_mm, f + 1)
                    if first(f):
                        dve.wait_ge(consts_ok, 1)
                    step = nc.vector.tensor_copy(logit[:, 0:E], ps_logit)
                elif link == 1:
                    step = nc.vector.max(out=top8[:, :], in_=ps_logit)
                elif link == 2:
                    after_links(2)
                    step = nc.vector.memset(top8[:, TOPK:8], LOW)
                elif link == 3:
                    after_links(3)
                    step = ts(half_max[:, :], top8[:, 0:1], -0.5, None, ALU.mult)
                elif link == 4:
                    step = nc.vector.match_replace(out=marked[:, :], in_to_replace=top8[:, :], in_values=logit[:, :],
                                                   imm_value=HIGH)
                elif link == 5:
                    dve.wait_ge(tz_ok, f + 1)
                    step = ts(ez_den[:, :], tz[:, :], -1.0, 1.0, ALU.mult, ALU.add)
                elif link == 6:
                    after_links(6)
                    step = nc.vector.reciprocal(ez_rec[:, :], ez_den[:, :])
                elif link == 7:
                    after_links(7)
                    step = stt(out=ez[:, :], in0=tz[:, :], scalar=1.0, in1=ez_rec[:, :], op0=ALU.add, op1=ALU.mult)
                elif link == 8:
                    after_links(8)
                    step = stt(out=ez_top[:, :], in0=marked[:, 0:E], scalar=HIGH, in1=ez[:, :], op0=ALU.is_ge,
                               op1=ALU.mult, accum_out=ez_sum[:, :])
                elif link == 9:
                    after_links(9)
                    step = nc.vector.reciprocal(ez_inv[:, :], ez_sum[:, :])
                else:
                    if not first(f):
                        dve.wait_ge(hid_ok, NG * f - 1)
                    after_links(10)
                    step = ts(comb[:, :], ez_top[:, :], ez_inv[:, 0:1], CSCALE, ALU.mult, ALU.mult)
                step.then_inc(route_step, 1)

            def hidden(f, g, j):
                if j == 0:
                    dve.wait_ge(silu_ok, NG * f + g + 1)
                    dve.wait_ge(up_mm, NG * f + g + 1)
                    if g == 0:
                        dve.wait_ge(route_step, LINKS * (f + 1))
                e, a, b = segments(g)[j]
                last = stt(out=hid[:, g, a:b], in0=up_bank(g)[:, a:b],
                           scalar=CSCALE if e is None else comb[:, e:e + 1], in1=silu_slot(g)[:, a:b],
                           op0=ALU.mult, op1=ALU.mult)
                if j == len(segments(g)) - 1:
                    last.then_inc(hid_ok, 1)

            def hidden_low(f, g, j):
                if j == 0:
                    dve.wait_ge(hhi_ok, NG * f + g + 1)
                half = slice(j * GC // 2, (j + 1) * GC // 2)
                tt(hid_lo[:, g, half], hid[:, g, half], hid_hi[:, g, half], ALU.subtract).then_inc(hlo_ok, 1)

            def finish(f, j):
                if j == 0:
                    dve.wait_ge(down_mm, NG * (f + 1))
                    tt(part[:, :], ps_out[:, H:2 * H], x_tok[:, f, :], ALU.add).then_inc(part_ok, 1)
                else:
                    dve.wait_ge(part_ok, f + 1)
                    tt(x_tok[:, f, :], ps_out[:, 0:H], part[:, :], ALU.add).then_inc(res_ok, 1)

            def ffn_work(f, items):
                for kind, g, j in items:
                    if kind == "product":
                        hidden(f, g, j)
                    elif kind == "low":
                        hidden_low(f, g, j)
                    elif kind == "route":
                        route(f, g)
                    else:
                        finish(f, j)

            def chunk(c, scan, ffn, pieces, before=True):
                for i in range(STG):
                    s, k = i // 4, i % 4
                    for piece in pieces[i]:
                        split_low(piece)
                    for n in range(max(len(VECTOR[i]), len(VECTOR[i + STG]))):
                        if ffn and before:
                            ffn_work(c - 2, VECTOR[i + STG][n:n + 1])
                        if ffn:
                            ffn_work(c - 1, VECTOR[i][n:n + 1])
                    if scan:
                        before_coupling(c, s, k)
                    if scan:
                        after_coupling(c, s, k)
                    if scan and i == STG - 1:
                        next_drive(c)

            chunk(0, True, False, LOW_PIECES[0])
            chunk(1, True, True, LOW_PIECES[1], before=False)
            chunk(2, True, True, LOW_PIECES[2])
            with dve.Fori(3, NC) as c:
                chunk(c, True, True, NO_PIECES)
            chunk(NC, False, True, NO_PIECES)
            for i in range(STG, 2 * STG):
                ffn_work(NC - 1, VECTOR[i])

        @block.tensor
        def _(pe):
            mm = nc.tensor.matmul

            def x_transposed(c):
                if c == 0:
                    pe.wait_ge(x0_in, 16 * SPC)
                elif c == 1:
                    pe.wait_ge(x_in, 16 * SPC)
                if c >= 4:
                    pe.wait_ge(drive_ok, NH * (c - 3))
                for n in range(NH):
                    last = nc.tensor.transpose(ps_xT(c, n), x_tok[:, c, n * P:(n + 1) * P], identf[:, :])
                last.then_inc(xT_mm, 1)

            def logits(f):
                for n in range(NH):
                    last = mm(ps_logit, q_new[:, n, :, :].rearrange("p s b -> p (s b)"), router[:, n, :],
                              start=(n == 0), stop=(n == NH - 1))
                last.then_inc(logit_mm, 1)

            def couple(c, s, k, route):
                n = c * STG + 4 * s + k
                pe.wait_ge(th_hi_ok, n + 1)
                if route == "logits":
                    logits(c - 1)
                elif route == "picked":
                    pe.wait_ge(route_step, LINKS * (c - 1) + 2)
                for m in range(NH):
                    to = slice(m * P, (m + 1) * P)
                    acc = ps_scan[:, m * B:(m + 1) * B]
                    mm(acc, coup_hi[:, 0, to], th_hi[:, 0, :], start=True, stop=False)
                    mm(acc, coup_hi[:, 1, to], th_hi[:, 1, :], start=False, stop=False)
                    mm(acc, coup_lo[:, 0, to], th_hi[:, 0, :], start=False, stop=False)
                    mm(acc, coup_lo[:, 1, to], th_hi[:, 1, :], start=False, stop=False)
                    pe.wait_ge(th_lo_ok, n + 1)
                    mm(acc, coup_hi[:, 0, to], th_lo[:, 0, :], start=False, stop=False)
                    last = mm(acc, coup_hi[:, 1, to], th_lo[:, 1, :], start=False, stop=True)
                last.then_inc(coupled, 1)

            def project(ps, hi, lo, g, i):
                n, term = i // 3, i % 3
                tok, w = ((tok_hi, hi), (tok_hi, lo), (tok_lo, hi))[term]
                return mm(ps[:, :], tok[:, n, :], w[:, n, g * GC:(g + 1) * GC], start=(i == 0), stop=(i == 3 * NH - 1))

            def unit(f, kind, g, i):
                n = NG * f + g
                if kind == "gate":
                    if i == 0:
                        if g == 0:
                            pe.wait_ge(tok_ok, 2 * (f + 1))
                        if first(f):
                            pe.wait_ge(w_lo_ok, split_for_group(g))
                        if g >= 2:
                            pe.wait_ge(silu_ok, n - 1)
                        elif g == 0 and not first(f):
                            pe.wait_ge(silu_ok, n)
                    last = project(ps_gate[g % 2], wg_hi, wg_lo, g, i)
                    if i == 3 * NH - 1:
                        last.then_inc(gate_mm, 1)
                elif kind == "up":
                    if i == 0:
                        if 2 <= g < NG - 1:
                            pe.wait_ge(hid_ok, n - 1)
                        elif g < 2 and not first(f):
                            pe.wait_ge(hid_ok, n - 2)
                    last = project(up_bank(g), wu_hi, wu_lo, g, i)
                    if i == 3 * NH - 1:
                        last.then_inc(up_mm, 1)
                elif kind == "turn":
                    pe.wait_ge(hlo_ok, 2 * (n + 1))
                    if g > 0 or not first(f):
                        pe.wait_ge(hidT_ok, 2 * n)
                    for t in range(2 * GT):
                        src = (hid_hi, hid_lo)[t // GT][:, g, t % GT * P:(t % GT + 1) * P]
                        last = nc.tensor.transpose(ps_hidT[:, t, :], src, ident16[:, :])
                    last.then_inc(hidT_mm, 1)
                else:
                    if i == 0:
                        pe.wait_ge(hidT_ok, 2 * (n + 1))
                        if g == 0 and not first(f):
                            pe.wait_ge(res_ok, f)
                    tile, final = g * GT + i, g == NG - 1 and i == GT - 1
                    if first(f):
                        pe.wait_ge(w_lo_ok, split_for_tile(tile))
                    mm(ps_out[:, :], hidT[:, g, i, :], wd[:, tile, :, :].rearrange("p a h -> p (a h)"),
                       start=(g == 0 and i == 0), stop=False, skip_group_check=True)
                    last = mm(ps_out[:, H:2 * H], hidT[:, g, GT + i, :], wd[:, tile, 0, :],
                              start=False, stop=final, skip_group_check=True)
                    if i == GT - 1:
                        last.then_inc(down_mm, 1)

            def chunk(c, scan, ffn, before=True):
                if ffn and first(c - 1):
                    pe.wait_ge(router_in, 16)
                    pe.wait_ge(drive_ok, NH * NC)
                for i in range(STG):
                    s, k = i // 4, i % 4
                    if scan and not ffn and i > STG - NC:
                        x_transposed(i - (STG - NC))
                    if scan:
                        couple(c, s, k, {ROUTE_PICK - 1: "logits", ROUTE_PICK: "picked"}.get(i) if ffn else None)
                    elif ffn and i == ROUTE_PICK - 1:
                        pe.wait_ge(y_ok, NC * STG + 1)
                        logits(c - 1)
                    if ffn and before:
                        for kind, g, j in MATRIX[i + STG]:
                            unit(c - 2, kind, g, j)
                    if ffn:
                        for kind, g, j in MATRIX[i]:
                            unit(c - 1, kind, g, j)

            pe.wait_ge(ident_ok, 2)
            pe.wait_ge(coup_in, 16)
            for n in range(NH):
                for m in range(NH):
                    last = nc.tensor.transpose(ps_gate[0][:, n * H + m * P:n * H + (m + 1) * P],
                                               coup_row[:, m, n * P:(n + 1) * P], identf[:, :])
            last.then_inc(coup_mm, 1)
            pe.wait_ge(cond_in, 16)
            for n in range(NH):
                last = nc.tensor.transpose(ps_scan[:, n * B:(n + 1) * B], cond_row[:, n * P:(n + 1) * P],
                                           identf[0:B, 0:B])
            last.then_inc(cond_mm, 1)
            pe.wait_ge(bias_in, 16)
            nc.tensor.transpose(ps_up[2][:, 0:NH], bias_row[:, :], identf[0:NH, 0:NH]).then_inc(bias_mm, 1)
            x_transposed(0)
            pe.wait_ge(coup_lo_ok, 1)
            pe.wait_ge(p0_ok, 1)

            chunk(0, True, False)
            chunk(1, True, True, before=False)
            chunk(2, True, True)
            with pe.Fori(3, NC) as c:
                chunk(c, True, True)
            chunk(NC, False, True)
            for i in range(STG, 2 * STG):
                for kind, g, j in MATRIX[i]:
                    unit(NC - 1, kind, g, j)


_INS = ["x", "cond_2048", "L0_cond_coupling", "L0_cond_bias", "L0_ffn_router_w", "L0_ffn_w_gate", "L0_ffn_w_up",
        "L0_ffn_w_down", "L0_ffn_ws_gate", "L0_ffn_ws_up", "L0_ffn_ws_down"]
_OUTS = [((B, T, H), "float32")]


def kernel(**inputs):
    import numpy as _np
    import concourse.bacc as _bacc
    from concourse import mybir as _mybir
    from concourse.bass_utils import run_bass_kernel_spmd as _run

    nc = _bacc.Bacc("TRN2", target_bir_lowering=False, num_devices=1)
    arrays, args = {}, []
    for name in _INS:
        a = _np.ascontiguousarray(inputs[name])
        arrays[f"in_{name}_dram"] = a
        args.append(nc.dram_tensor(f"in_{name}_dram", a.shape, _mybir.dt.from_np(a.dtype), kind="ExternalInput").ap())
    for i, (shape, dtype) in enumerate(_OUTS):
        dt = _mybir.dt.from_np(_np.dtype(dtype))
        args.append(nc.dram_tensor(f"out_{i}_dram", shape, dt, kind="ExternalOutput").ap())
    build(nc, *args)
    r = _run(nc, [arrays], core_ids=[0])
    return r.results[0]["out_0_dram"]
```
